# Optimizing a Trainium2 kernel written in Bass

```python
import numpy as np
import jax
import jax.numpy as jnp

def _softmax(x, axis=-1):
    return jax.nn.softmax(x, axis=axis)

def _gelu(x):
    return jax.nn.gelu(x, approximate=True)

def _silu(x):
    return jax.nn.silu(x)

def _sigmoid(x):
    return jax.nn.sigmoid(x)

def _layernorm(x, axis=-1, eps=1e-05):
    m = jnp.mean(x, axis=axis, keepdims=True)
    v = jnp.var(x, axis=axis, keepdims=True)
    return (x - m) / jnp.sqrt(v + eps)

def _scatter_add(tgt, idx, src, axis=0):
    return tgt.at[idx].add(src)

def _segment_sum(src, seg, n):
    return jax.ops.segment_sum(src, seg, n)
kernel_name = 'mk_cond_resid_d2_seqx_r8_1e30e5'

def setup_inputs(seed: int=0):
    np.random.seed(seed)
    _w = jnp.asarray

    def _rec_inputs():
        import jax
        import jax.numpy as jnp
        _rk = jax.random.key(seed)
        x = -7.109e-05 + 0.9999 * jax.random.normal(jax.random.fold_in(_rk, 1), (32, 32, 256), jnp.float32)
        _lenS = 32 - jax.random.randint(jax.random.fold_in(_rk, 7), (32,), 0, max(1, 32 // 4) + 1, jnp.int32)
        _lenS2 = 32 - jax.random.randint(jax.random.fold_in(_rk, 8), (32,), 0, max(1, 32 // 4) + 1, jnp.int32)
        itok_B_1_198 = jax.random.randint(jax.random.fold_in(_rk, 11), (32,), 1, 199, jnp.int32)
        itok_Bx257_0_4111 = jax.random.randint(jax.random.fold_in(_rk, 12), (32, 257), 0, 514, jnp.int32)
        itok_B_37_3939 = jax.random.randint(jax.random.fold_in(_rk, 13), (32,), 37, 3940, jnp.int32)
        return (x, itok_B_1_198, itok_Bx257_0_4111, itok_B_37_3939)
    x, itok_B_1_198, itok_Bx257_0_4111, itok_B_37_3939 = _rec_inputs()

    def _L0_cond_setup():
        import jax, jax.numpy as jnp
        import numpy as np
        B, C, T = (128, 32, 256)
        S, D = (200, 32)
        key = jax.random.key(seed)
        k1, k2, k3 = jax.random.split(key, 3)
        x = jax.random.normal(k1, (B, C, T), dtype=jnp.float32)
        conditions = jax.random.randint(k2, (B,), 0, S, dtype=jnp.int64)
        weights = jax.random.normal(k3, (S, C, D), dtype=jnp.float32) / jnp.sqrt(jnp.float32(C))
        return {'x': x, 'conditions': conditions, 'weights': weights}
    _L0_cond_all = _L0_cond_setup()
    _L0_cond_in = {k: v for k, v in _L0_cond_all.items() if k in ('weights',)}
    del _L0_cond_all

    def _L1_cond_setup():
        import jax, jax.numpy as jnp
        import numpy as np
        H, G, HD = (8, 4, 32)
        GSZ = H // G
        BLOCK = 16
        WINDOW = 128
        SCALE = 256.0 ** (-0.5)
        EPS = 1e-06
        THETA = 10000.0
        B, T, D = (16, 4, 256)
        NBLK = 257

        def _rms(x, scale):
            var = jnp.mean(x * x, axis=-1, keepdims=True)
            return x * jax.lax.rsqrt(var + EPS) * (1.0 + scale)

        def _rope(x, pos):
            half = HD // 2
            inv = 1.0 / THETA ** (jnp.arange(half, dtype=jnp.float32) / half)
            ang = pos[:, :, None].astype(jnp.float32) * inv
            cos = jnp.cos(ang)[:, None, :, :]
            sin = jnp.sin(ang)[:, None, :, :]
            x1, x2 = (x[..., :half], x[..., half:])
            return jnp.concatenate([x1 * cos - x2 * sin, x2 * cos + x1 * sin], axis=-1)
        key = jax.random.key(seed)
        ks = jax.random.split(key, 10)
        inv_d = 1.0 / np.sqrt(D)
        return {'x': jax.random.normal(ks[0], (B, T, D), jnp.float32), 'Wq': jax.random.normal(ks[1], (H * HD, D), jnp.float32) * inv_d, 'Wk': jax.random.normal(ks[2], (G * HD, D), jnp.float32) * inv_d, 'Wv': jax.random.normal(ks[3], (G * HD, D), jnp.float32) * inv_d, 'Wo': jax.random.normal(ks[4], (D, H * HD), jnp.float32) * inv_d, 'q_norm_scale': jax.random.normal(ks[5], (HD,), jnp.float32) * 0.02, 'k_norm_scale': jax.random.normal(ks[6], (HD,), jnp.float32) * 0.02, 'k_blocks': jax.random.normal(ks[7], (B * NBLK, G, BLOCK, HD), jnp.float32), 'v_blocks': jax.random.normal(ks[8], (B * NBLK, G, BLOCK, HD), jnp.float32), 'block_tables': jnp.arange(B * NBLK, dtype=jnp.int32).reshape(B, NBLK), 'kv_lens': jax.random.randint(ks[9], (B,), 0, 512, dtype=jnp.int32)}
    _L1_cond_all = _L1_cond_setup()
    _L1_cond_in = {k: v for k, v in _L1_cond_all.items() if k in ('Wq', 'Wk', 'Wv', 'Wo', 'q_norm_scale', 'k_norm_scale', 'k_blocks', 'v_blocks')}
    del _L1_cond_all
    return {'x': x, 'itok_B_1_198': itok_B_1_198, 'itok_Bx257_0_4111': itok_Bx257_0_4111, 'itok_B_37_3939': itok_B_37_3939, 'L0_cond_weights': _L0_cond_in['weights'], 'L1_cond_Wq': _L1_cond_in['Wq'], 'L1_cond_Wk': _L1_cond_in['Wk'], 'L1_cond_Wv': _L1_cond_in['Wv'], 'L1_cond_Wo': _L1_cond_in['Wo'], 'L1_cond_q_norm_scale': _L1_cond_in['q_norm_scale'], 'L1_cond_k_norm_scale': _L1_cond_in['k_norm_scale'], 'L1_cond_k_blocks': _L1_cond_in['k_blocks'], 'L1_cond_v_blocks': _L1_cond_in['v_blocks']}

def reference(x, itok_B_1_198, itok_Bx257_0_4111, itok_B_37_3939, L0_cond_weights, L1_cond_Wq, L1_cond_Wk, L1_cond_Wv, L1_cond_Wo, L1_cond_q_norm_scale, L1_cond_k_norm_scale, L1_cond_k_blocks, L1_cond_v_blocks):
    import jax
    import jax.numpy as jnp

    def _L0_cond_ref(x, conditions, weights):
        import jax, jax.numpy as jnp
        import numpy as np
        B, C, T = (128, 32, 256)
        S, D = (200, 32)
        w = weights[conditions]
        return jnp.einsum('bct,bcd->bdt', x, w)

    def _L1_cond_ref(x, Wq, Wk, Wv, Wo, q_norm_scale, k_norm_scale, k_blocks, v_blocks, block_tables, kv_lens):
        import jax, jax.numpy as jnp
        import numpy as np
        H, G, HD = (8, 4, 32)
        GSZ = H // G
        BLOCK = 16
        WINDOW = 128
        SCALE = 256.0 ** (-0.5)
        EPS = 1e-06
        THETA = 10000.0
        B, T, D = (16, 4, 256)
        NBLK = 257

        def _rms(x, scale):
            var = jnp.mean(x * x, axis=-1, keepdims=True)
            return x * jax.lax.rsqrt(var + EPS) * (1.0 + scale)

        def _rope(x, pos):
            half = HD // 2
            inv = 1.0 / THETA ** (jnp.arange(half, dtype=jnp.float32) / half)
            ang = pos[:, :, None].astype(jnp.float32) * inv
            cos = jnp.cos(ang)[:, None, :, :]
            sin = jnp.sin(ang)[:, None, :, :]
            x1, x2 = (x[..., :half], x[..., half:])
            return jnp.concatenate([x1 * cos - x2 * sin, x2 * cos + x1 * sin], axis=-1)
        Bx, Tx, _ = x.shape
        q = jnp.einsum('btd,od->bto', x, Wq).reshape(Bx, Tx, H, HD).transpose(0, 2, 1, 3)
        k = jnp.einsum('btd,od->bto', x, Wk).reshape(Bx, Tx, G, HD).transpose(0, 2, 1, 3)
        v = jnp.einsum('btd,od->bto', x, Wv).reshape(Bx, Tx, G, HD).transpose(0, 2, 1, 3)
        q = _rms(q, q_norm_scale)
        k = _rms(k, k_norm_scale)
        pos = kv_lens[:, None] + jnp.arange(Tx, dtype=jnp.int32)
        q = _rope(q, pos)
        k = _rope(k, pos)
        slot = pos // BLOCK
        off = pos % BLOCK
        blk = jnp.take_along_axis(block_tables, slot, axis=1)
        k_blocks = k_blocks.at[blk, :, off, :].set(k.transpose(0, 2, 1, 3))
        v_blocks = v_blocks.at[blk, :, off, :].set(v.transpose(0, 2, 1, 3))
        k_all = k_blocks[block_tables].transpose(0, 2, 1, 3, 4).reshape(Bx, G, -1, HD)
        v_all = v_blocks[block_tables].transpose(0, 2, 1, 3, 4).reshape(Bx, G, -1, HD)
        S = k_all.shape[2]
        qg = q.reshape(Bx, G, GSZ, Tx, HD)
        scores = jnp.einsum('bghtd,bgsd->bghts', qg, k_all) * SCALE
        kpos = jnp.arange(S, dtype=jnp.int32)
        allowed = (kpos[None, None, :] <= pos[:, :, None]) & (kpos[None, None, :] > pos[:, :, None] - WINDOW)
        scores = jnp.where(allowed[:, None, None, :, :], scores, -jnp.inf)
        p = jax.nn.softmax(scores, axis=-1)
        o = jnp.einsum('bghts,bgsd->bghtd', p, v_all).reshape(Bx, H, Tx, HD)
        o = o.transpose(0, 2, 1, 3).reshape(Bx, Tx, H * HD)
        return jnp.einsum('bto,do->btd', o, Wo)
    x = x + _L0_cond_ref(x, itok_B_1_198, L0_cond_weights)
    x = x + _L1_cond_ref(x, L1_cond_Wq, L1_cond_Wk, L1_cond_Wv, L1_cond_Wo, L1_cond_q_norm_scale, L1_cond_k_norm_scale, L1_cond_k_blocks, L1_cond_v_blocks, itok_Bx257_0_4111, itok_B_37_3939)
    return x

_drawn_inputs = setup_inputs


def setup_inputs(seed=0):
    import zlib

    import numpy as np

    out = dict(_drawn_inputs(seed))
    spreads = {}
    factors = {'L1_cond_Wk': 11.963,
     'L1_cond_q_norm_scale': 28.298,
     'L1_cond_k_norm_scale': 64.0,
     'L1_cond_k_blocks': 2.777}
    for name, (base, spread) in spreads.items():
        noise = np.random.default_rng([zlib.crc32(name.encode()), seed]).standard_normal(out[name].shape)
        drawn = base * np.exp(spread * noise) if base else spread * noise
        out[name] = jnp.asarray(drawn.astype(out[name].dtype))
    for name, factor in factors.items():
        out[name] = (out[name] * factor).astype(out[name].dtype)
    return out
```

```python
from contextlib import ExitStack

import concourse.bass as bass
import numpy as np
from concourse import mybir

F32 = mybir.dt.float32
BF16 = mybir.dt.bfloat16
I32 = mybir.dt.int32
ALU = mybir.AluOpType
ACT = mybir.ActivationFunctionType
AX_X = mybir.AxisListType.X

P = 128
B, T, D = 32, 32, 256
H, G, HD = 8, 4, 32
HH = H // G
BLOCK, NBLK, NPOOL = 16, 257, 4112
WINDOW = 128
SCALE = float(D) ** -0.5
EPS, THETA = 1e-6, 10000.0
GD = G * HD
BB = P // T
NT = B // BB
NS = 11
SP_ = NS * BLOCK
HS = SP_ // 2
KK = P // B
WS = 3
NJ = B * WS
RB_ = [11, 11, 10]
R0 = [0, 11, 22]
NR = RB_[0] * NS
NRT = len(RB_)
V0 = [(j % 2) * 2 * RB_[0] for j in range(NRT)]
K0 = [(j % 2) * RB_[0] * SP_ for j in range(NRT)]
QK = (H + G) * HD
NW = (H + 2 * G) * HD
ROWF = 2 * GD
BIG = 1.0e6
NEG = -1.0e30
MAGIC = 12582912.0
C1 = 6.28125
C2 = float(np.float32(np.round((2 * np.pi - C1) * 2 ** 21) / 2 ** 21))
C3 = float(np.float32(2 * np.pi - C1 - C2))
PI_ = 3.1415925

CONST_COLS = [("ident", P), ("ones", P), ("slot_of", 4), ("iota", NBLK), ("pick_w", NT * 6), ("pick_j", NJ),
              ("pick_r", B * NS), ("row_of", P), ("jp1", NJ), ("off16", BLOCK), ("tcol", 1), ("own_j", NT),
              ("k3", WS), ("jrow", SP_), ("bd", BB), ("gmask", P), ("hsel", HH * T), ("invf", HD // 2), ("eps", 1)]
CONST_AT = {}
_at = 0
for _name, _n in CONST_COLS:
    CONST_AT[_name] = (_at, _n)
    _at += _n
NCONST = _at
MERGE_AT = [0, 3, 14]
KEYS_AT = [0, 6, 17]
NEARLY = CONST_AT["jrow"][0]


def constants():
    p = np.arange(P)
    kk, b = p // B, p % B
    c = {}
    c["ident"] = np.eye(P)
    c["ones"] = np.ones((P, P))
    c["slot_of"] = np.stack([4 * 0 + kk, 4 + kk, 8 + kk, kk], 1)
    c["iota"] = np.tile(np.arange(NBLK), (P, 1))
    pw = np.zeros((P, NT, 6))
    for n in range(NT):
        for v in range(6):
            pw[:, n, v] = (b // BB == n) & (kk == (0 if v < 3 else v - 3))
    c["pick_w"] = pw.reshape(P, -1)
    j = np.arange(NJ)
    c["pick_j"] = (b[:, None] == j // WS) & (kk[:, None] == j % WS)
    r = np.arange(B * NS)
    c["pick_r"] = (b[:, None] == r // NS) & (kk[:, None] == r % NS % KK)
    c["row_of"] = b[:, None] % BB == p[None, :] // T
    c["jp1"] = np.tile(j + 1, (P, 1))
    c["off16"] = np.tile(np.arange(BLOCK), (P, 1))
    c["tcol"] = (p % T)[:, None]
    c["own_j"] = WS * (BB * np.arange(NT)[None, :] + p[:, None] // T) + 1
    c["k3"] = np.tile(np.arange(WS), (P, 1))
    c["jrow"] = np.arange(SP_)[None, :] - (p % T)[:, None] + 63.5
    c["bd"] = p[:, None] // T == np.arange(BB)[None, :]
    c["gmask"] = (p[:, None] // 64) == (p[None, :] % 64) // HD
    c["hsel"] = p[:, None] % 64 == np.arange(64)[None, :]
    c["invf"] = np.tile(1.0 / THETA ** (np.arange(HD // 2) / (HD // 2)), (P, 1))
    c["eps"] = np.full((P, 1), EPS)
    return np.concatenate([np.asarray(c[n], np.float32) for n, _ in CONST_COLS], 1)


def selectors():
    k, m = np.arange(P), np.arange(P)
    s = [(k[:, None] // T == j) & (k[:, None] % T == m[None, :] % T) for j in range(BB)]
    return np.concatenate(s, 1).astype(np.float32)


def build(nc, x, meta, w0, w_all, wo_t, scales, kb, vb, consts, sel, out, new_tab, v_tab):
    with ExitStack() as ctx:
        def sb(name, shape, dt=F32):
            return ctx.enter_context(nc.sbuf_tensor(name, shape, dt))

        def sem(name):
            return ctx.enter_context(nc.semaphore(name))

        cst = sb("cst", [P, NCONST])

        def const(name):
            a, n = CONST_AT[name]
            return cst[:, a:a + n]

        ident, ones = const("ident"), const("ones")

        meta_i = sb("meta_i", [P, NBLK + 2], I32)
        meta_f = sb("meta_f", [P, NBLK + 2])
        tab, kv, cond = meta_f[:, 0:NBLK], meta_f[:, NBLK:NBLK + 1], meta_f[:, NBLK + 1:NBLK + 2]
        scratch = sb("scratch", [P, 2 * NT * NJ])
        hit = scratch[:, 0:NBLK]
        ix = sb("ix", [P, 16])
        base = sb("base", [P, 4])
        found = sb("found", [P, 4])
        vals = sb("vals", [P, 6])
        mv_w = sb("mv_w", [P, NT, 6])
        mv_j = sb("mv_j", [P, 3, NJ])
        mv_r = sb("mv_r", [P, B + 1, NS])
        w6 = sb("w6", [P, NT, 6])
        jcol = sb("jcol", [P, 3])
        blk_rf = sb("blk_rf", [NR, NRT])
        rows_j = sb("rows_j", [P, 3, NJ])
        blk_ri = sb("blk_ri", [NR, NRT], I32)
        cond_i = sb("cond_i", [P, NT], I32)
        cnt_rf = sb("cnt_rf", [NR, NRT])
        new_ri = sb("new_ri", [NR, NRT], I32)
        match = sb("match", [NJ, B, NS])
        cover = sb("cover", [NJ, BLOCK])
        cmp_a = scratch[:, 0:NT * NJ].rearrange("p (n j) -> p n j", j=NJ)
        cmp_b = scratch[:, NT * NJ:].rearrange("p (n j) -> p n j", j=NJ)
        wq8 = sb("wq8", [P, 12, NT])
        wk3 = sb("wk3", [P, NT, WS])
        dst_i = sb("dst_i", [P, NT], I32)
        mask_c = sb("mask_c", [P, NT])
        sq_m = sb("sq_m", [P, 2, SP_])
        mask = sb("mask", [P, NT, SP_], BF16)
        selb = sb("selb", [P, BB, P], BF16)

        ang = sb("ang", [P, NT, HD // 2])
        turn = sb("turn", [P, NT, HD // 2])
        sin_ = sb("sin_", [P, NT, HD // 2])
        cos_ = sb("cos_", [P, NT, HD // 2])
        scl = sb("scl", [P, 2, HD])
        ga = sb("ga", [P, 2, HD])
        gb = sb("gb", [P, 2, HD])
        t1 = sb("t1", [P, 2, NT, HD])
        t2 = sb("t2", [P, 2, NT, HD])

        xs = sb("xs", [P, NT, D])
        x1 = xs
        wg = sb("wg", [P, NT, T])
        wbd = sb("wbd", [P, 2, BB, T])
        xt = sb("xt", [P, 2, 2, P])
        w_sb = sb("w_sb", [P, 2, NW])
        wo_sb = sb("wo_sb", [P, HH, D])
        row_tmp = sb("row_tmp", [P, 5, QK])
        qk = row_tmp[:, 0:2, :]
        sq, ra, rb = row_tmp[:, 2, :], row_tmp[:, 3, :], row_tmp[:, 4, :]
        row_flat = row_tmp[:].rearrange("p a b -> p (a b)")
        ms = sb("ms", [P, H + G])
        rt = sb("rt", [P, H + G])
        rstd = sb("rstd", [P, H + G])
        rq = sb("rq", [P, 2, H * HD])
        new = sb("new", [P, NT, ROWF])
        qbd = sb("qbd", [P, B, 2, P])

        k_old = sb("k_old", [P, 2, G * BLOCK * HD])
        v_old = sb("v_old", [P, 2, G * BLOCK * HD])
        mrg = sb("mrg", [P, 2, BLOCK, ROWF])
        kt = sb("kt", [P, 2 * RB_[0] * SP_])
        vs = sb("vs", [HS, 2 * 2 * RB_[0], GD])

        pr = scratch[:, 0:3 * 2 * SP_].rearrange("p (c a s) -> p c a s", c=3, a=2)
        pts = sb("pts", [HS, 2, 2, 2, P])
        nmx = sb("nmx", [P, 3, 2])
        sums = sb("sums", [P, 3, 2])
        rin = sb("rin", [P, 3, 2])
        amat = sb("amat", [P, 2, P])
        r_sb = row_flat[:, 0:512].rearrange("p (a b) -> p a b", a=2)
        ot = row_flat[:, 512:1024].rearrange("p (h n b t) -> p h n b t", h=HH, n=2, b=BB)
        yo = row_flat[:, 1024:1536].rearrange("p (n d) -> p n d", n=2)

        bank = [ctx.enter_context(nc.psum_tensor(f"bank{i}", [P, 512], F32)) for i in range(8)]
        p_ix = bank[1]
        p_rr = bank[7][:, 0:B * NS]
        p_x1, p_xt, p_qkv, p_qt = [bank[0], bank[2]], [bank[3], bank[6]], [bank[4], bank[5]], bank[7]
        p_s, p_pt, p_or = [bank[2], bank[3]], [bank[6], bank[7]], [bank[0], bank[5]]

        def p_k(j, q):
            return bank[5] if j == 0 and q % 2 else bank[4]

        p_rj = p_ix[:, 0:3 * NJ]
        p_br = p_ix[0:NR, 288:288 + NRT]
        p_jc = p_ix[0:NJ, 292:295]
        p_w6 = p_ix[:, 296:296 + NT * 6]
        p_ct = p_ix[:, 344:344 + NRT * BLOCK]
        p_keep = p_ix[:, 392:392 + NRT * BLOCK]

        s_meta = sem("s_meta"); s_c1 = sem("s_c1"); s_c2 = sem("s_c2"); s_x = sem("s_x"); s_w = sem("s_w")
        s_wo = sem("s_wo"); s_scl = sem("s_scl"); s_sel = sem("s_sel")
        s_dve = sem("s_dve"); s_act = sem("s_act"); s_pool = sem("s_pool")
        s_mv = sem("s_mv")
        s_ix = sem("s_ix")
        s_gi = sem("s_gi")
        s_nri = sem("s_nri"); s_mat = sem("s_mat"); s_cnt = sem("s_cnt"); s_keep = sem("s_keep")
        s_dst = sem("s_dst"); s_mc = sem("s_mc"); s_msq = sem("s_msq"); s_msk = sem("s_msk")
        s_ang = sem("s_ang"); s_trig = sem("s_trig")
        s_zero = sem("s_zero"); s_zr1 = sem("s_zr1"); s_init = sem("s_init")
        s_wg = [sem(f"s_wg{i}") for i in range(NT)]
        s_k = [sem(f"s_k{i}") for i in range(NRT)]
        s_v = [sem(f"s_v{i}") for i in range(NRT)]
        s_wbd = sem("s_wbd"); s_px1 = sem("s_px1"); s_x1 = sem("s_x1"); s_pxt = sem("s_pxt"); s_xt = sem("s_xt")
        s_pq = sem("s_pq"); s_sq = sem("s_sq"); s_ms = sem("s_ms"); s_rt = sem("s_rt"); s_vc = sem("s_vc")
        s_rot = sem("s_rot"); s_pqt = sem("s_pqt"); s_qz = sem("s_qz"); s_qbd = sem("s_qbd"); s_qfree = sem("s_qfree")
        s_sc = sem("s_sc")
        s_n = [sem(f"s_n{i}") for i in range(NRT)]
        s_mv_ = sem("s_mrg_v"); s_mk = sem("s_mrg_k")
        s_vst = sem("s_vst")
        s_vs = [sem(f"s_vs{i}") for i in range(NRT)]
        s_pk = sem("s_pk"); s_kt = sem("s_kt")
        s_ps = sem("s_ps"); s_nmx = sem("s_nmx"); s_pr = sem("s_pr"); s_ppt = sem("s_ppt"); s_pts = sem("s_pts")
        s_am = sem("s_am"); s_po = sem("s_po"); s_r = sem("s_r"); s_ot = sem("s_ot"); s_py = sem("s_py")
        s_y = sem("s_y"); s_out = [sem("s_out0"), sem("s_out1")]

        block = ctx.enter_context(nc.Block())

        @block.sync
        def _(sp):
            sp.dma_start(meta_i[:], meta).then_inc(s_meta, 16)
            sp.dma_start(cst[:, 0:NEARLY], consts[:, 0:NEARLY]).then_inc(s_c1, 16)
            sp.dma_start(xs[:], x.rearrange("(n b) t d -> (b t) n d", b=BB)).then_inc(s_x, 16)
            sp.dma_start(cst[:, NEARLY:], consts[:, NEARLY:]).then_inc(s_c2, 16)
            sp.dma_start(w_sb[:], w_all.rearrange("(h p) n -> p h n", p=P)).then_inc(s_w, 16)
            sp.dma_start(scl[:], scales.rearrange("p (a b) -> p a b", a=2)).then_inc(s_scl, 16)
            sp.dma_start(selb[:].rearrange("p a b -> p (a b)"), sel).then_inc(s_sel, 16)
            sp.dma_start(wo_sb[:], wo_t.rearrange("(h p) n -> p h n", p=P)).then_inc(s_wo, 16)
            sp.wait_ge(s_zero, 1)
            sp.dma_start(new_tab.rearrange("(j o) f -> j (o f)", o=BLOCK),
                         mrg[0:NJ, 0, :, :].rearrange("p o f -> p (o f)")).then_inc(s_init, 16)
            for j in range(NRT):
                n = RB_[j] * NS
                sp.wait_ge(s_mv_, j + 1)
                sp.dma_start(v_tab[R0[j] * SP_:(R0[j] + RB_[j]) * SP_, :].rearrange("(r o) f -> r o f", o=BLOCK),
                             mrg[0:n, j % 2, :, GD:]).then_inc(s_vst, 16)
                sp.wait_ge(s_vst, 16 * (j + 1))
                if j >= 2:
                    sp.wait_ge(s_po, R0[j - 1])
                sp.dma_start(vs[:, V0[j]:V0[j] + 2 * RB_[j], :],
                             v_tab[R0[j] * SP_:(R0[j] + RB_[j]) * SP_, :].rearrange("(r p) f -> p r f", p=HS)
                             ).then_inc(s_vs[j], 16)
            out_v = out.rearrange("(n b) t d -> n (b t) d", b=BB)
            for n in range(NT):
                sp.wait_ge(s_y, n + 1)
                sp.dma_start(out_v[n], yo[:, n % 2, :]).then_inc(s_out[n % 2], 16)
            for i in range(2):
                sp.wait_ge(s_out[i], 16 * (NT // 2))

        @block.gpsimd
        def _(pool):
            nc.gpsimd.memset(mrg[:, 0], 0.0).then_inc(s_zero, 1)
            pool.wait_ge(s_gi, 1)
            def gather_w(n):
                pool.indirect_dma_start(wg[:, n, :], None, w0, bass.IndirectOffsetOnAxis(ap=cond_i[:, n:n + 1], axis=0),
                                        bounds_check=200 * T - 1, oob_is_err=False).then_inc(s_wg[n], 16)

            def gather_old(dst, src, j, s):
                n = RB_[j] * NS
                pool.indirect_dma_start(dst[0:n, j % 2, :], None, src.rearrange("n g o d -> n (g o d)"),
                                        bass.IndirectOffsetOnAxis(ap=blk_ri[0:n, j:j + 1], axis=0),
                                        bounds_check=NPOOL - 1, oob_is_err=False).then_inc(s, 16)

            for n in range(NT):
                gather_w(n)
                if n == 3:
                    gather_old(v_old, vb, 0, s_v[0])
                    gather_old(k_old, kb, 0, s_k[0])
            nc.gpsimd.memset(mrg[:, 1], 0.0).then_inc(s_zr1, 1)
            gather_old(v_old, vb, 1, s_v[1])
            gather_old(k_old, kb, 1, s_k[1])
            pool.wait_ge(s_dst, 1)
            pool.wait_ge(s_init, 16)
            for n in range(NT):
                pool.wait_ge(s_msq, n + 1)
                nc.gpsimd.tensor_scalar(mask[:, n, :], sq_m[:, n % 2, :], 64.0 * 64.0, NEG, ALU.is_gt, ALU.mult
                                        ).then_inc(s_msk, 1)
                pool.wait_ge(s_rot, n + 1)
                pool.wait_ge(s_vc, n + 1)
                pool.indirect_dma_start(new_tab, bass.IndirectOffsetOnAxis(ap=dst_i[:, n:n + 1], axis=0),
                                        new[:, n, :], None,
                                        bounds_check=NJ * BLOCK - 1, oob_is_err=False).then_inc(s_sc, 16)
                if n == 0:
                    pool.wait_ge(s_zr1, 1)
            pool.wait_ge(s_sc, 16 * NT)
            pool.wait_ge(s_nri, 1)
            for j in range(NRT):
                n = RB_[j] * NS
                if j >= 2:
                    pool.wait_ge(s_pk, 4 * (j - 1))
                    pool.wait_ge(s_vst, 16 * (j - 1))
                pool.indirect_dma_start(mrg[0:n, j % 2, :, :].rearrange("p o f -> p (o f)"), None,
                                        new_tab.rearrange("(j o) f -> j (o f)", o=BLOCK),
                                        bass.IndirectOffsetOnAxis(ap=new_ri[0:n, j:j + 1], axis=0),
                                        bounds_check=NJ - 1, oob_is_err=False).then_inc(s_n[j], 16)
                if j == 1:
                    pool.wait_ge(s_mv_, 1)
                    gather_old(v_old, vb, 2, s_v[2])
                    pool.wait_ge(s_mk, 1)
                    gather_old(k_old, kb, 2, s_k[2])

        @block.vector
        def _(dve):
            steps = [0]
            V = nc.vector

            def link(ins):
                steps[0] += 1
                ins.then_inc(s_dve, 1)
                dve.wait_ge(s_dve, steps[0])

            V.memset(mv_r[:, B, :], 0.0)
            dve.wait_ge(s_meta, 16)
            link(V.tensor_copy(meta_f[:], meta_i[:]))
            dve.wait_ge(s_c1, 16)
            link(V.tensor_scalar(ix[:, 0:1], kv, 1.0 / BLOCK, -(WINDOW - 1) / BLOCK - 15 / 32, ALU.mult, ALU.add))
            link(V.tensor_scalar(ix[:, 1:2], kv, 1.0 / BLOCK, -15 / 32, ALU.mult, ALU.add))
            link(V.tensor_scalar(ix[:, 0:2], ix[:, 0:2], MAGIC, None, ALU.add))
            link(V.tensor_scalar(ix[:, 0:2], ix[:, 0:2], MAGIC, None, ALU.subtract))
            link(V.tensor_scalar(ix[:, 0:1], ix[:, 0:1], 0.0, None, ALU.max))
            V.tensor_scalar(base[:, 0:3], const("slot_of")[:, 0:3], ix[:, 0:1], None, ALU.add)
            link(V.tensor_scalar(base[:, 3:4], const("slot_of")[:, 3:4], ix[:, 1:2], None, ALU.add))
            for i in range(4):
                link(V.scalar_tensor_tensor(out=hit, in0=const("iota"), scalar=base[:, i:i + 1], in1=tab,
                                            op0=ALU.is_equal, op1=ALU.mult, accum_out=found[:, i:i + 1]))
            pick_r = const("pick_r").rearrange("p (b s) -> p b s", s=NS)
            V.tensor_tensor(mv_r[:, 0:B, 0:2 * KK].rearrange("p b (i k) -> p b i k", k=KK),
                            pick_r[:, :, 0:2 * KK].rearrange("p b (i k) -> p b i k", k=KK),
                            found[:, 0:2].unsqueeze(1).unsqueeze(3).broadcast_to([P, B, 2, KK]), ALU.mult)
            link(V.tensor_tensor(mv_r[:, 0:B, 2 * KK:NS], pick_r[:, :, 2 * KK:NS],
                                 found[:, 2:3].unsqueeze(2).broadcast_to([P, B, NS - 2 * KK]), ALU.mult))
            V.tensor_copy(vals[:, 0:1], kv)
            V.tensor_copy(vals[:, 1:2], cond)
            V.tensor_copy(vals[:, 2:3], ix[:, 0:1])
            link(V.tensor_copy(vals[:, 3:6], found[:, 3:4].broadcast_to([P, 3])))
            V.tensor_tensor(mv_w[:], const("pick_w").rearrange("p (n v) -> p n v", v=6),
                            vals[:].unsqueeze(1).broadcast_to([P, NT, 6]), ALU.mult).then_inc(s_mv, 1)
            link(V.scalar_tensor_tensor(out=ix[:, 2:3], in0=base[:, 3:4], scalar=-float(BLOCK), in1=kv,
                                        op0=ALU.mult, op1=ALU.add))
            link(V.tensor_scalar(ix[:, 3:4], ix[:, 2:3], float(T), float(BLOCK), ALU.add, ALU.min))
            link(V.tensor_scalar(ix[:, 4:5], ix[:, 2:3], 0.0, float(BLOCK), ALU.max, ALU.min))
            link(V.tensor_scalar(ix[:, 5:6], ix[:, 3:4], 0.0, None, ALU.max))
            link(V.scalar_tensor_tensor(out=ix[:, 6:8], in0=found[:, 3:4].broadcast_to([P, 2]), scalar=float(BLOCK),
                                        in1=ix[:, 4:6], op0=ALU.mult, op1=ALU.add))
            V.tensor_scalar(mv_j[:, 0, :], const("pick_j"), found[:, 3:4], None, ALU.mult)
            V.tensor_scalar(mv_j[:, 1, :], const("pick_j"), ix[:, 6:7], None, ALU.mult)
            V.tensor_scalar(mv_j[:, 2, :], const("pick_j"), ix[:, 7:8], None, ALU.mult)
            link(V.tensor_copy(ix[:, 8:9], found[:, 3:4]))
            V.tensor_copy(ix[:, 9:11], ix[:, 4:6]).then_inc(s_mv, 1)
            dve.wait_ge(s_ix, 1)
            V.tensor_copy(blk_ri[:], p_br)
            V.tensor_copy(blk_rf[:], p_br)
            link(V.tensor_copy(w6[:], p_w6.rearrange("p (n v) -> p n v", v=6)))
            link(V.tensor_scalar(wq8[:, 0, :], w6[:, :, 1], float(T), const("tcol"), ALU.mult, ALU.add))
            V.tensor_copy(cond_i[:], wq8[:, 0, :]).then_inc(s_gi, 1)
            link(V.tensor_scalar(wq8[:, 1, :], w6[:, :, 0], const("tcol"), None, ALU.add))
            dve.wait_ge(s_c2, 16)
            link(V.tensor_tensor(ang[:], wq8[:, 1, :].unsqueeze(2).broadcast_to([P, NT, HD // 2]),
                                 const("invf").unsqueeze(1).broadcast_to([P, NT, HD // 2]), ALU.mult))
            link(V.tensor_scalar(turn[:], ang[:], 1.0 / (2 * np.pi), MAGIC, ALU.mult, ALU.add))
            link(V.tensor_scalar(turn[:], turn[:], MAGIC, None, ALU.subtract))
            for c in (C1, C2, C3):
                link(V.scalar_tensor_tensor(out=ang[:], in0=turn[:], scalar=-c, in1=ang[:], op0=ALU.mult, op1=ALU.add))
            V.tensor_scalar(ang[:], ang[:], PI_, -PI_, ALU.min, ALU.max).then_inc(s_ang, 1)
            V.scalar_tensor_tensor(out=mask_c[:], in0=w6[:, :, 2], scalar=float(BLOCK), in1=w6[:, :, 0],
                                   op0=ALU.mult, op1=ALU.subtract).then_inc(s_mc, 1)
            dve.wait_ge(s_scl, 16)
            link(V.tensor_scalar(ga[:], scl[:], 1.0, None, ALU.add))
            link(V.tensor_scalar(ga[:, 0, :], ga[:, 0, :], SCALE, None, ALU.mult))
            V.tensor_copy(gb[:, :, 16:32], ga[:, :, 0:16])
            link(V.tensor_scalar(gb[:, :, 0:16], ga[:, :, 16:32], -1.0, None, ALU.mult))
            dve.wait_ge(s_trig, 1)
            link(V.tensor_scalar(cos_[:], cos_[:], -2.0, 1.0, ALU.mult, ALU.add))
            for a in range(2):
                for tt, gg, tr in ((t1, ga, cos_), (t2, gb, sin_)):
                    last = V.tensor_tensor(tt[:, a].rearrange("p n (h i) -> p n h i", h=2),
                                           gg[:, a].rearrange("p (h i) -> p h i", h=2).unsqueeze(1).broadcast_to([P, NT, 2, 16]),
                                           tr[:].unsqueeze(2).broadcast_to([P, NT, 2, 16]), ALU.mult)
            link(last)

            def wbd_tile(n):
                dve.wait_ge(s_wg[n], 16)
                if n >= 2:
                    dve.wait_ge(s_px1, n - 1)
                V.tensor_tensor(wbd[:, n % 2], wg[:, n, :].unsqueeze(1).broadcast_to([P, BB, T]),
                                const("bd").unsqueeze(2).broadcast_to([P, BB, T]), ALU.mult).then_inc(s_wbd, 1)

            def x1_tile(n):
                dve.wait_ge(s_px1, n + 1)
                V.tensor_tensor(x1[:, n, :], p_x1[n % 2][:, 0:D], xs[:, n, :], ALU.add).then_inc(s_x1, 1)

            def rot_tile(n):
                px = qk[:, n % 2, :].rearrange("p (h d) -> p h d", d=HD)
                av = ra.rearrange("p (h d) -> p h d", d=HD)
                bv = rb.rearrange("p (h d) -> p h d", d=HD)
                if n >= 1:
                    dve.wait_ge(s_rot, n)
                dve.wait_ge(s_sq, n + 1)
                V.tensor_reduce(ms[:], sq.rearrange("p (h d) -> p h d", d=HD), AX_X, ALU.add).then_inc(s_ms, 1)
                for a, h0, h1 in ((0, 0, H), (1, H, H + G)):
                    V.tensor_tensor(av[:, h0:h1, :], px[:, h0:h1, :],
                                    t1[:, a, n, :].unsqueeze(1).broadcast_to([P, h1 - h0, HD]), ALU.mult)
                    V.tensor_tensor(bv[:, h0:h1, 0:16], px[:, h0:h1, 16:32],
                                    t2[:, a, n, 0:16].unsqueeze(1).broadcast_to([P, h1 - h0, 16]), ALU.mult)
                    last = V.tensor_tensor(bv[:, h0:h1, 16:32], px[:, h0:h1, 0:16],
                                           t2[:, a, n, 16:32].unsqueeze(1).broadcast_to([P, h1 - h0, 16]), ALU.mult)
                link(last)
                link(V.tensor_tensor(ra, ra, rb, ALU.add))
                dve.wait_ge(s_rt, n + 1)
                link(V.reciprocal(rstd[:], rt[:]))
                if n >= 2:
                    dve.wait_ge(s_pqt, n - 1)
                V.tensor_tensor(rq[:, n % 2, :].rearrange("p (h d) -> p h d", d=HD), av[:, 0:H, :],
                                rstd[:, 0:H].unsqueeze(2).broadcast_to([P, H, HD]), ALU.mult)
                V.tensor_tensor(new[:, n, 0:GD].rearrange("p (h d) -> p h d", d=HD), av[:, H:H + G, :],
                                rstd[:, H:H + G].unsqueeze(2).broadcast_to([P, G, HD]), ALU.mult).then_inc(s_rot, 1)

            def readers_index():
                V.tensor_copy(rows_j[:], p_rj.rearrange("p (a j) -> p a j", a=3))
                link(V.tensor_copy(jcol[0:NJ, :], p_jc))
                link(V.tensor_tensor(cmp_a[0:NR, 0:NRT, :], rows_j[0:NR, 0, :].unsqueeze(1).broadcast_to([NR, NRT, NJ]),
                                     blk_rf[:].unsqueeze(2).broadcast_to([NR, NRT, NJ]), ALU.is_equal))
                link(V.tensor_tensor(cmp_a[0:NR, 0:NRT, :], cmp_a[0:NR, 0:NRT, :],
                                     const("jp1")[0:NR].unsqueeze(1).broadcast_to([NR, NRT, NJ]), ALU.mult))
                link(V.tensor_reduce(cnt_rf[:], cmp_a[0:NR, 0:NRT, :], AX_X, ALU.max))
                link(V.tensor_scalar(blk_rf[:], cnt_rf[:], 0.0, BIG, ALU.is_equal, ALU.mult))
                link(V.scalar_tensor_tensor(out=blk_rf[:], in0=cnt_rf[:], scalar=-1.0, in1=blk_rf[:],
                                            op0=ALU.add, op1=ALU.add))
                V.tensor_copy(new_ri[:], blk_rf[:]).then_inc(s_nri, 1)
                V.tensor_scalar(match[:], p_rr[0:NJ].rearrange("p (b s) -> p b s", s=NS), jcol[0:NJ, 0:1], None, ALU.is_equal)
                V.tensor_scalar(cmp_b[0:NJ, 0, 0:BLOCK], const("off16")[0:NJ], jcol[0:NJ, 1:2], None, ALU.is_ge)
                link(V.tensor_scalar(cmp_b[0:NJ, 1, 0:BLOCK], const("off16")[0:NJ], jcol[0:NJ, 2:3], None, ALU.is_lt))
                V.tensor_tensor(cover[:], cmp_b[0:NJ, 0, 0:BLOCK], cmp_b[0:NJ, 1, 0:BLOCK], ALU.mult).then_inc(s_mat, 1)
                dve.wait_ge(s_cnt, 1)
                for j in range(NRT):
                    n = RB_[j] * NS
                    last = V.tensor_scalar(p_keep[0:n, j * BLOCK:(j + 1) * BLOCK].bitcast(I32),
                                           p_ct[0:n, j * BLOCK:(j + 1) * BLOCK], 0.0, None, ALU.is_equal)
                link(last)

            def writers_index():
                q = lambda i: wq8[:, i, :]
                jb = [P, NT, NJ]
                V.tensor_scalar(q(2), w6[:, :, 0], 1.0 / BLOCK, -15 / 32, ALU.mult, ALU.add)
                link(V.tensor_scalar(q(3), q(1), 1.0 / BLOCK, -15 / 32, ALU.mult, ALU.add))
                link(V.tensor_scalar(wq8[:, 2:4, :], wq8[:, 2:4, :], MAGIC, None, ALU.add))
                link(V.tensor_scalar(wq8[:, 2:4, :], wq8[:, 2:4, :], MAGIC, None, ALU.subtract))
                V.tensor_tensor(q(4), q(3), q(2), ALU.subtract)
                link(V.scalar_tensor_tensor(out=q(5), in0=q(3), scalar=-float(BLOCK), in1=q(1), op0=ALU.mult, op1=ALU.add))
                link(V.tensor_tensor(wk3[:], q(4).unsqueeze(2).broadcast_to([P, NT, WS]),
                                     const("k3").unsqueeze(1).broadcast_to([P, NT, WS]), ALU.is_equal))
                link(V.tensor_tensor(wk3[:], wk3[:], w6[:, :, 3:6], ALU.mult))
                link(V.tensor_reduce(q(6), wk3[:], AX_X, ALU.add))
                link(V.scalar_tensor_tensor(out=q(7), in0=q(6), scalar=float(BLOCK), in1=q(5), op0=ALU.mult, op1=ALU.add))
                V.tensor_tensor(cmp_a, q(7).unsqueeze(2).broadcast_to(jb), rows_j[:, 1, :].unsqueeze(1).broadcast_to(jb), ALU.is_ge)
                link(V.tensor_tensor(cmp_b, q(7).unsqueeze(2).broadcast_to(jb), rows_j[:, 2, :].unsqueeze(1).broadcast_to(jb), ALU.is_lt))
                link(V.tensor_tensor(cmp_a, cmp_a, cmp_b, ALU.mult))
                link(V.tensor_tensor(cmp_a, cmp_a, const("jp1").unsqueeze(1).broadcast_to(jb), ALU.mult))
                link(V.tensor_reduce(q(8), cmp_a, AX_X, ALU.max))
                link(V.tensor_tensor(cmp_b, q(6).unsqueeze(2).broadcast_to(jb), rows_j[:, 0, :].unsqueeze(1).broadcast_to(jb), ALU.is_equal))
                link(V.tensor_tensor(cmp_b, cmp_b, const("jp1").unsqueeze(1).broadcast_to(jb), ALU.mult))
                link(V.tensor_reduce(q(9), cmp_b, AX_X, ALU.max))
                link(V.tensor_tensor(q(10), q(4), const("own_j"), ALU.add))
                link(V.tensor_tensor(q(10), q(10), q(8), ALU.not_equal))
                link(V.scalar_tensor_tensor(out=q(11), in0=q(9), scalar=float(BLOCK), in1=q(5), op0=ALU.mult, op1=ALU.add))
                link(V.tensor_scalar(q(11), q(11), float(BLOCK), None, ALU.subtract))
                link(V.scalar_tensor_tensor(out=q(11), in0=q(10), scalar=BIG, in1=q(11), op0=ALU.mult, op1=ALU.add))
                V.tensor_copy(dst_i[:], q(11)).then_inc(s_dst, 1)

            wbd_tile(0)
            wbd_tile(1)
            readers_index()
            for i in range(NT + 2):
                if i < NT:
                    x1_tile(i)
                    if i + 2 < NT:
                        wbd_tile(i + 2)
                if i == 1:
                    writers_index()
                if i >= 2:
                    rot_tile(i - 2)

            def merge(j, old, s_old, f0, s_done):
                n = RB_[j] * NS
                dve.wait_ge(s_old, 16)
                dve.wait_ge(s_n[j], 16)
                dst = mrg[0:n, j % 2, :, f0:f0 + GD].rearrange("p o (g d) -> p o g d", d=HD)
                keep = p_keep[0:n, j * BLOCK:(j + 1) * BLOCK].bitcast(I32).unsqueeze(2).unsqueeze(3).broadcast_to([n, BLOCK, G, HD])
                V.copy_predicated(dst, keep, old[0:n, j % 2, :].rearrange("p (g o d) -> p o g d", g=G, d=HD)).then_inc(s_done, 1)

            def rows_out(n):
                dve.wait_ge(s_py, n + 1)
                if n >= 2:
                    dve.wait_ge(s_out[n % 2], 16 * (n // 2))
                V.tensor_tensor(yo[:, n % 2, :], p_or[n % 2][:, 0:D], x1[:, n, :], ALU.add).then_inc(s_y, 1)

            for b in range(B + 4):
                if b in MERGE_AT:
                    j = MERGE_AT.index(b)
                    merge(j, v_old, s_v[j], GD, s_mv_)
                    merge(j, k_old, s_k[j], 0, s_mk)
                if b < B:
                    dve.wait_ge(s_ps, b + 1)
                    if b >= 3:
                        dve.wait_ge(s_pr, 2 * (b - 2))
                    V.tensor_reduce(nmx[:, b % 3, :], p_s[b % 2][:, 0:2 * SP_].rearrange("p (a s) -> p a s", a=2), AX_X,
                                    ALU.max, negate=True).then_inc(s_nmx, 1)
                c = b - 1
                if 0 <= c < B:
                    dve.wait_ge(s_pr, 2 * c + 2)
                    link(V.reciprocal(rin[:, c % 3, :], sums[:, c % 3, :]))
                    if c >= 2:
                        dve.wait_ge(s_po, c - 1)
                    V.tensor_tensor(amat[:, c % 2, :].rearrange("p (a f) -> p a f", a=2),
                                    const("gmask").rearrange("p (a f) -> p a f", a=2),
                                    rin[:, c % 3, :].unsqueeze(2).broadcast_to([P, 2, 64]), ALU.mult).then_inc(s_am, 1)
                    dve.wait_ge(s_ppt, c + 1)
                    V.tensor_copy(pts[:, c % 2].rearrange("p a b f -> p (a b f)"), p_pt[c % 2][0:HS, :]).then_inc(s_pts, 1)
                k = (b - BB - 2) // BB
                if b >= BB + 2 and b % BB == 2 and k < NT:
                    dve.wait_ge(s_r, k + 1)
                    if k >= 2:
                        dve.wait_ge(s_py, k - 1)
                    V.tensor_tensor(ot[:, :, k % 2].rearrange("p h b t -> p b h t"),
                                    p_or[k % 2][:, 0:256].rearrange("p (b h t) -> p b h t", b=BB, h=HH),
                                    r_sb[:, k % 2, :].rearrange("p (b h t) -> p b h t", b=BB, h=HH), ALU.mult).then_inc(s_ot, 1)
                if b >= 2 * BB and b % BB == 0:
                    rows_out(b // BB - 2)
            rows_out(NT - 1)

        @block.scalar
        def _(act):
            steps = [0]
            A = nc.scalar

            def link(ins):
                steps[0] += 1
                ins.then_inc(s_act, 1)
                act.wait_ge(s_act, steps[0])

            A.memzero(qbd[:].rearrange("p b a f -> p (b a f)")).then_inc(s_qz, 1)
            act.wait_ge(s_ang, 1)
            A.activation(sin_[:], ang[:], ACT.Sin)
            link(A.activation(cos_[:], ang[:], ACT.Sin, scale=0.5))
            A.activation(cos_[:], cos_[:], ACT.Square).then_inc(s_trig, 1)
            act.wait_ge(s_mc, 1)

            def window(n):
                if n >= 2:
                    act.wait_ge(s_msk, n - 1)
                A.activation(sq_m[:, n % 2, :], const("jrow"), ACT.Square, bias=mask_c[:, n:n + 1]).then_inc(s_msq, 1)

            window(0)
            window(1)
            for i in range(NT + 4):
                if 2 <= i < NT:
                    window(i)
                if i < NT:
                    act.wait_ge(s_pxt, i + 1)
                    if i >= 2:
                        act.wait_ge(s_pq, i - 1)
                    A.activation(xt[:, i % 2].rearrange("p h f -> p (h f)"), p_xt[i % 2][:, 0:2 * P],
                                 ACT.Copy).then_inc(s_xt, 1)
                n = i - 1
                if 0 <= n < NT:
                    act.wait_ge(s_pq, n + 1)
                    if n >= 2:
                        act.wait_ge(s_rot, n - 1)
                    link(A.activation(qk[:, n % 2, :], p_qkv[n % 2][:, 0:QK], ACT.Copy))
                    A.activation(new[:, n, GD:], p_qkv[n % 2][:, QK:NW], ACT.Copy).then_inc(s_vc, 1)
                    if n >= 1:
                        act.wait_ge(s_ms, n)
                    A.activation(sq, qk[:, n % 2, :], ACT.Square).then_inc(s_sq, 1)
                    act.wait_ge(s_ms, n + 1)
                    if n >= 1:
                        act.wait_ge(s_rot, n)
                    A.activation(rt[:], ms[:], ACT.Sqrt, scale=1.0 / HD, bias=const("eps")).then_inc(s_rt, 1)
                m = i - 3
                if 0 <= m < NT:
                    act.wait_ge(s_pqt, m + 1)
                    if m == 0:
                        act.wait_ge(s_qz, 1)
                    for g in range(G):
                        last = A.activation(
                            qbd[HD * g:HD * (g + 1), BB * m:BB * (m + 1), g // 2, (g % 2) * 64:(g % 2) * 64 + 64
                                ].rearrange("p b (h t) -> p b h t", h=HH),
                            p_qt[HD * g:HD * (g + 1), 0:HH * P].rearrange("p (h b t) -> p b h t", h=HH, b=BB), ACT.Copy)
                    last.then_inc(s_qbd, 1)

            def keys(j, q=None):
                n = RB_[j] * NS
                if j >= 2:
                    act.wait_ge(s_ps, R0[j - 1])
                for q in (range(4) if q is None else [q]):
                    act.wait_ge(s_pk, 4 * j + q + 1)
                    A.activation(kt[:, K0[j]:K0[j] + RB_[j] * SP_].rearrange("p (r o) -> p r o", o=BLOCK)[:, :, 4 * q:4 * q + 4],
                                 p_k(j, q)[:, 0:4 * n].rearrange("p (o r) -> p r o", o=4), ACT.Copy).then_inc(s_kt, 1)

            for b in range(B + 4):
                for j, at in enumerate(KEYS_AT):
                    if j == 0 and b == 0:
                        keys(0)
                    elif j and at <= b < at + 4:
                        keys(j, b - at)
                if b < B:
                    act.wait_ge(s_nmx, b + 1)
                    if b >= 3:
                        act.wait_ge(s_ppt, b - 2)
                        act.wait_ge(s_am, b - 2)
                    for a in range(2):
                        A.activation(pr[:, b % 3, a, :], p_s[b % 2][:, a * SP_:(a + 1) * SP_], ACT.Exp,
                                     bias=nmx[:, b % 3, a:a + 1], accum_out=sums[:, b % 3, a:a + 1]).then_inc(s_pr, 1)
                k = (b - BB - 2) // BB
                if b >= BB + 2 and b % BB == 2 and k < NT:
                    act.wait_ge(s_po, BB * (k + 1))
                    if k >= 2:
                        act.wait_ge(s_ot, k - 1)
                    A.activation(r_sb[:, k % 2, :], p_or[k % 2][:, 256:512], ACT.Copy).then_inc(s_r, 1)

        @block.tensor
        def _(pe):
            mm = pe.matmul
            pe.wait_ge(s_c1, 16)
            pe.wait_ge(s_mv, 2)
            for j in range(NRT):
                mm(p_br[:, j:j + 1], mv_r[:, R0[j]:R0[j] + RB_[0], :].rearrange("p b s -> p (b s)"), ones[:, 0:1], start=True, stop=True)
            mm(p_w6, const("row_of"), mv_w[:].rearrange("p n v -> p (n v)"), start=True, stop=True)
            for a in range(3):
                mm(p_jc[:, a:a + 1], const("pick_j"), ix[:, 8 + a:9 + a], start=True, stop=True)
            mm(p_rj, ones, mv_j[:].rearrange("p a j -> p (a j)"), start=True, stop=True)
            mm(p_rr, ones, mv_r[:, 0:B, :].rearrange("p b s -> p (b s)"), start=True, stop=True).then_inc(s_ix, 1)

            pe.wait_ge(s_x, 16)
            for i in range(NT + 4):
                if i < NT:
                    pe.wait_ge(s_wbd, i + 1)
                    if i >= 2:
                        pe.wait_ge(s_x1, i - 1)
                    mm(p_x1[i % 2][:, 0:D], wbd[:, i % 2].rearrange("p b t -> p (b t)"), xs[:, i, :],
                       start=True, stop=True).then_inc(s_px1, 1)
                if i == 1:
                    pe.wait_ge(s_mat, 1)
                    for j in range(NRT):
                        last = mm(p_ct[0:RB_[j] * NS, j * BLOCK:(j + 1) * BLOCK], match[:, R0[j]:R0[j] + RB_[j], :].rearrange("p b s -> p (b s)"), cover[:],
                                  start=True, stop=True)
                    last.then_inc(s_cnt, 1)
                n = i - 1
                if 0 <= n < NT:
                    pe.wait_ge(s_x1, n + 1)
                    if n >= 2:
                        pe.wait_ge(s_xt, n - 1)
                    for h in range(2):
                        last = pe.transpose(p_xt[n % 2][:, h * P:(h + 1) * P],
                                            x1[:, n, h * P:(h + 1) * P], ident)
                    last.then_inc(s_pxt, 1)
                n = i - 2
                if 0 <= n < NT:
                    pe.wait_ge(s_xt, n + 1)
                    if n == 0:
                        pe.wait_ge(s_w, 16)
                    if n >= 2:
                        pe.wait_ge(s_vc, n - 1)
                    for h in range(2):
                        last = mm(p_qkv[n % 2][:, :], xt[:, n % 2, h, :], w_sb[:, h, :], start=(h == 0), stop=(h == 1))
                    last.then_inc(s_pq, 1)
                n = i - 4
                if 0 <= n < NT:
                    pe.wait_ge(s_rot, n + 1)
                    if n >= 1:
                        pe.wait_ge(s_qbd, n)
                    for h in range(HH):
                        last = pe.transpose(p_qt[:, h * P:(h + 1) * P],
                                            rq[:, n % 2, h * P:(h + 1) * P], ident)
                    last.then_inc(s_pqt, 1)

            def keys(j, q):
                n = RB_[j] * NS
                pe.wait_ge(s_mk, j + 1)
                if 4 * j + q >= 2:
                    pe.wait_ge(s_kt, 4 * j + q - (1 if j == 0 else 0))
                for o in range(4):
                    last = pe.transpose(p_k(j, q)[:, o * n:(o + 1) * n], mrg[0:n, j % 2, 4 * q + o, 0:GD], ident[0:n, 0:n])
                last.then_inc(s_pk, 1)

            pe.wait_ge(s_vc, NT)
            for q in range(4):
                keys(0, q)
            for b in range(B + 4):
                for j, at in enumerate(KEYS_AT):
                    if j and at <= b < at + 4:
                        keys(j, b - at)
                if b < B:
                    if b == 0:
                        pe.wait_ge(s_sel, 16)
                        pe.wait_ge(s_msk, NT)
                        pe.wait_ge(s_qbd, NT)
                    if b in R0:
                        pe.wait_ge(s_kt, 4 * (R0.index(b) + 1))
                    if b >= 2:
                        pe.wait_ge(s_pr, 2 * (b - 1))
                    tj = b // RB_[0]
                    k0 = K0[tj] + (b - R0[tj]) * SP_
                    for a in range(2):
                        o = p_s[b % 2][:, a * SP_:(a + 1) * SP_]
                        mm(o, qbd[:, b, a, :], kt[:, k0:k0 + SP_], start=True, stop=False)
                        last = mm(o, selb[:, b % BB, :], mask[:, b // BB, :], start=False, stop=True)
                    last.then_inc(s_ps, 1)
                c = b - 1
                if 0 <= c < B:
                    pe.wait_ge(s_pr, 2 * c + 2)
                    if c >= 2:
                        pe.wait_ge(s_pts, c - 1)
                    for hf in range(2):
                        for a in range(2):
                            k = 2 * hf + a
                            last = pe.transpose(p_pt[c % 2][0:HS, k * P:(k + 1) * P], pr[:, c % 3, a, hf * HS:(hf + 1) * HS], ident)
                    last.then_inc(s_ppt, 1)
                e = b - 2
                if 0 <= e < B:
                    pe.wait_ge(s_pts, e + 1)
                    pe.wait_ge(s_am, e + 1)
                    if e in R0:
                        pe.wait_ge(s_vs[R0.index(e)], 16)
                    k = e // BB
                    if e == BB:
                        pe.wait_ge(s_kt, 4)
                    if e % BB == 0 and k >= 2:
                        pe.wait_ge(s_y, k - 1)
                    o0 = (e % BB) * 64
                    tj = e // RB_[0]
                    v0 = V0[tj] + 2 * (e - R0[tj])
                    for g in range(G):
                        for hf in range(2):
                            mm(p_or[k % 2][HD * g:HD * (g + 1), o0:o0 + 64], vs[:, v0 + hf, HD * g:HD * (g + 1)],
                               pts[:, e % 2, hf, g // 2, (g % 2) * 64:(g % 2) * 64 + 64], start=(hf == 0), stop=(hf == 1))
                    mm(p_or[k % 2][:, o0 + 256:o0 + 320], amat[:, e % 2, :], const("hsel"), start=True, stop=True).then_inc(s_po, 1)
                f = b - 4
                if f >= 0 and f % BB == BB - 1:
                    n = f // BB
                    pe.wait_ge(s_ot, n + 1)
                    if n == 0:
                        pe.wait_ge(s_wo, 16)
                    for h in range(HH):
                        last = mm(p_or[n % 2][:, 0:D], ot[:, h, n % 2].rearrange("p b t -> p (b t)"),
                                  wo_sb[:, h, :], start=(h == 0), stop=(h == HH - 1))
                    last.then_inc(s_py, 1)


def kernel(**inputs):
    import numpy as _np
    import concourse.bacc as _bacc
    from concourse import mybir as _mybir
    from ml_dtypes import bfloat16 as _bf16
    from concourse.bass_utils import run_bass_kernel_spmd as _run

    g = {k: _np.ascontiguousarray(v) for k, v in inputs.items()}
    wq = g["L1_cond_Wq"].reshape(G, HH, HD, D).transpose(1, 0, 2, 3).reshape(H * HD, D)
    wo = g["L1_cond_Wo"].reshape(D, G, HH, HD).transpose(2, 1, 3, 0).reshape(H * HD, D)
    w_all = _np.concatenate([wq, g["L1_cond_Wk"], g["L1_cond_Wv"]], 0).T
    meta = _np.concatenate([g["itok_Bx257_0_4111"], g["itok_B_37_3939"][:, None], g["itok_B_1_198"][:, None]], 1)
    arrays = {
        "x": g["x"],
        "meta": _np.tile(meta, (KK, 1)),
        "w0": g["L0_cond_weights"].reshape(200 * T, T),
        "w_all": w_all,
        "wo_t": wo,
        "scales": _np.tile(_np.concatenate([g["L1_cond_q_norm_scale"], g["L1_cond_k_norm_scale"]])[None], (P, 1)),
        "kb": g["L1_cond_k_blocks"],
        "vb": g["L1_cond_v_blocks"],
        "consts": constants(),
        "sel": selectors().astype(_bf16),
    }
    arrays = {"in_" + k: _np.ascontiguousarray(v) for k, v in arrays.items()}
    nc = _bacc.Bacc("TRN2", target_bir_lowering=False, num_devices=1)
    args = [nc.dram_tensor(k, a.shape, _mybir.dt.from_np(a.dtype), kind="ExternalInput").ap() for k, a in arrays.items()]
    args.append(nc.dram_tensor("out_0", (B, T, D), F32, kind="ExternalOutput").ap())
    args.append(nc.dram_tensor("new_tab", (NJ * BLOCK, ROWF), F32, kind="Internal").ap())
    args.append(nc.dram_tensor("v_tab", (B * SP_, GD), F32, kind="Internal").ap())
    build(nc, *args)
    r = _run(nc, [arrays], core_ids=[0])
    return r.results[0]["out_0"]
```

```python
from contextlib import ExitStack

import concourse.bass as bass
import numpy as np
from concourse import mybir

F32 = mybir.dt.float32
BF16 = mybir.dt.bfloat16
I32 = mybir.dt.int32
ALU = mybir.AluOpType
ACT = mybir.ActivationFunctionType
AX_X = mybir.AxisListType.X

P = 128
B, T, D = 32, 32, 256
H, G, HD = 8, 4, 32
HH = H // G
BLOCK, NBLK, NPOOL = 16, 257, 4112
WINDOW = 128
SCALE = float(D) ** -0.5
EPS, THETA = 1e-6, 10000.0
GD = G * HD
BB = P // T
NT = B // BB
NS = 11
SP_ = NS * BLOCK
HS = SP_ // 2
KK = P // B
WS = 3
NJ = B * WS
RB_ = [11, 11, 10]
R0 = [0, 11, 22]
NR = RB_[0] * NS
NRT = len(RB_)
NP_ = NT // 2
V0 = [(j % 2) * 2 * RB_[0] for j in range(NRT)]
K0 = [(j % 2) * RB_[0] * SP_ for j in range(NRT)]
QK = (H + G) * HD
NW = (H + 2 * G) * HD
ROWF = 2 * GD
BIG = 1.0e6
NEG = -1.0e30
MAGIC = 12582912.0
C1 = 6.28125
C2 = float(np.float32(np.round((2 * np.pi - C1) * 2 ** 21) / 2 ** 21))
C3 = float(np.float32(2 * np.pi - C1 - C2))
PI_ = 3.1415925

CONST_COLS = [("slot_of", 4), ("tcol", 1), ("iota", NBLK), ("ident", P), ("ones", P), ("pick_w", NT * WS),
              ("pick_r", B * NS), ("row_of", P), ("later", P), ("order", P), ("off16", BLOCK), ("cell", WS * BLOCK),
              ("bd", BB), ("jrow", SP_), ("gmask", P), ("hsel", HH * T), ("invf", HD // 2), ("eps", 1)]
CONST_AT = {}
_at = 0
for _name, _n in CONST_COLS:
    CONST_AT[_name] = (_at, _n)
    _at += _n
NCONST = _at
MERGE_V, MERGE_K = [0, 1, 11], [0, 2, 12]
KEYS_AT = {b: (1, (b - 3) // 2) for b in (3, 5, 7, 9)} | {b: (2, (b - 13) // 2) for b in (13, 15, 17, 19)}
NFIRST = CONST_AT["ident"][0]
NEARLY = CONST_AT["jrow"][0]


def constants():
    p = np.arange(P)
    kk, b = p // B, p % B
    c = {}
    c["ident"] = np.eye(P)
    c["ones"] = np.ones((P, P))
    c["slot_of"] = np.stack([4 * 0 + kk, 4 + kk, 8 + kk, kk], 1)
    c["iota"] = np.tile(np.arange(NBLK), (P, 1))
    pw = np.zeros((P, NT, WS))
    for n in range(NT):
        for v in range(WS):
            pw[:, n, v] = (b // BB == n) & (kk == v)
    c["pick_w"] = pw.reshape(P, -1)
    r = np.arange(B * NS)
    c["pick_r"] = (b[:, None] == r // NS) & (kk[:, None] == r % NS % KK)
    c["row_of"] = b[:, None] % BB == p[None, :] // T
    order = np.where(kk < WS, WS * b + kk + 1, 0)
    c["order"] = np.tile(order, (P, 1))
    c["later"] = (order[:, None] > order[None, :]) & (order[None, :] > 0)
    c["cell"] = np.tile(np.arange(WS * BLOCK), (P, 1))
    c["off16"] = np.tile(np.arange(BLOCK), (P, 1))
    c["tcol"] = (p % T)[:, None]
    c["jrow"] = np.arange(SP_)[None, :] - (p % T)[:, None] + 63.5
    c["bd"] = p[:, None] // T == np.arange(BB)[None, :]
    c["gmask"] = (p[:, None] // 64) == (p[None, :] % 64) // HD
    c["hsel"] = p[:, None] % 64 == np.arange(64)[None, :]
    c["invf"] = np.tile(1.0 / THETA ** (np.arange(HD // 2) / (HD // 2)), (P, 1))
    c["eps"] = np.full((P, 1), EPS)
    return np.concatenate([np.asarray(c[n], np.float32) for n, _ in CONST_COLS], 1)


def selectors():
    k, m = np.arange(P), np.arange(P)
    s = [(k[:, None] // T == j) & (k[:, None] % T == m[None, :] % T) for j in range(BB)]
    return np.concatenate(s, 1).astype(np.float32)


def build(nc, x, row_meta, tables, w0, w_all, wo_t, scales, kb, vb, consts, sel, out, new_tab, v_tab):
    with ExitStack() as ctx:
        def sb(name, shape, dt=F32):
            return ctx.enter_context(nc.sbuf_tensor(name, shape, dt))

        def sem(name):
            return ctx.enter_context(nc.semaphore(name))

        cst = sb("cst", [P, NCONST])

        def const(name):
            a, n = CONST_AT[name]
            return cst[:, a:a + n]

        ident, ones = const("ident"), const("ones")

        rm_i = sb("rm_i", [P, 2 * NT + 1], I32)
        rm = sb("rm", [P, 2 * NT + 1])
        kv_w, cond_w, kv = rm[:, 0:NT], rm[:, NT:2 * NT], rm[:, 2 * NT:2 * NT + 1]
        tab_i = sb("tab_i", [P, NBLK], I32)
        tab = sb("tab", [P, NBLK])
        scratch = sb("scratch", [P, 3 * NT * WS * BLOCK + NRT * P])
        ix = sb("ix", [P, 16])
        base = sb("base", [P, 4])
        found = sb("found", [P, 4])
        mv_w = sb("mv_w", [P, NT, WS])
        fl = sb("fl", [P, 3 * NT + 2])
        mv_j = sb("mv_j", [P, P])
        mv_r = sb("mv_r", [P, B + 1, NS])
        blk_rf = sb("blk_rf", [NR, NRT])
        rows_j = sb("rows_j", [P, P])
        blk_ri = sb("blk_ri", [NR, NRT], I32)
        cond_i = sb("cond_i", [P, NT], I32)
        cnt_rf = sb("cnt_rf", [NR, NRT])
        new_ri = sb("new_ri", [NR, NRT], I32)
        match = sb("match", [P, B, NS])
        cover = sb("cover", [P, BLOCK])
        cov_a = sb("cov_a", [P, 2, BLOCK])
        over = sb("over", [P, P])
        dcol = sb("dcol", [P, 2])
        dcell = sb("dcell", [P, 2, BLOCK])
        here = scratch[:, 0:NT * WS * BLOCK].rearrange("p (n c) -> p n c", c=WS * BLOCK)
        dwork = scratch[:, NT * WS * BLOCK:2 * NT * WS * BLOCK]
        dpick = scratch[:, 2 * NT * WS * BLOCK:3 * NT * WS * BLOCK]
        rwork = scratch[:, 3 * NT * WS * BLOCK:3 * NT * WS * BLOCK + NRT * P].rearrange("p (j c) -> p j c", c=P)
        wq8 = sb("wq8", [P, 4, NT])
        dst_i = sb("dst_i", [P, NT], I32)
        mask_c = sb("mask_c", [P, NT])
        sq_m = sb("sq_m", [P, 2, SP_])
        mask = sb("mask", [P, NT, SP_], BF16)
        selb = sb("selb", [P, BB, P], BF16)

        ang = sb("ang", [P, NT, HD // 2])
        turn = sb("turn", [P, NT, HD // 2])
        sin_ = sb("sin_", [P, NT, HD // 2])
        cos_ = sb("cos_", [P, NT, HD // 2])
        scl = sb("scl", [P, 2, HD])
        ga = sb("ga", [P, 2, HD])
        gb = sb("gb", [P, 2, HD])
        t1 = sb("t1", [P, 2, NT, HD])
        t2 = sb("t2", [P, 2, NT, HD])

        xs = sb("xs", [P, NT, D])
        x1 = xs
        wg = sb("wg", [P, NT, T])
        wbd = sb("wbd", [P, NT, BB, T])
        rows_kt = sb("rows_kt", [P, NT * D + NT * ROWF])
        xt = rows_kt[:, 0:NT * D].rearrange("p (n h f) -> p n h f", n=NT, h=2)
        new = rows_kt[:, NT * D:].rearrange("p (n f) -> p n f", f=ROWF)
        kt = rows_kt[:, 0:2 * RB_[0] * SP_]
        w_sb = sb("w_sb", [P, 2, NW])
        wo_sb = sb("wo_sb", [P, HH, D])
        sq = sb("sq", [P, 2 * H * HD])
        ra = sb("ra", [P, 2 * H * HD])
        rb = sb("rb", [P, 2 * H * HD])
        ms = sb("ms", [P, 2 * H])
        rt = sb("rt", [P, 2 * H])
        rstd = sb("rstd", [P, 2 * H])
        rq = sb("rq", [P, 2, 2 * H * HD])
        qbd = sb("qbd", [P, B, 2, P])

        k_old = sb("k_old", [P, 2, G * BLOCK * HD])
        v_old = sb("v_old", [P, 2, G * BLOCK * HD])
        mrg = sb("mrg", [P, 2, BLOCK, ROWF])
        vs = sb("vs", [HS, 2 * 2 * RB_[0], GD])

        pr = scratch[:, 0:3 * 2 * SP_].rearrange("p (c a s) -> p c a s", c=3, a=2)
        pts = sb("pts", [HS, 2, 2, 2, P])
        nmx = sb("nmx", [P, 3, 2])
        sums = sb("sums", [P, 3, 2])
        rin = sb("rin", [P, 3, 2])
        amat = sb("amat", [P, 2, P])
        r_sb = sb("r_sb", [P, 2, BB * HH * T])
        ot = sb("ot", [P, HH, 2, BB, T])
        yo = sb("yo", [P, 2, D])

        bank = [ctx.enter_context(nc.psum_tensor(f"bank{i}", [P, 512], F32)) for i in range(8)]
        p_ix = bank[1]
        p_rr = bank[7][:, 0:B * NS]
        p_xt, p_kv = [bank[2], bank[3]], [bank[4], bank[5]]
        p_q, p_qt, p_xr = [bank[2], bank[3]], [bank[6], bank[7]], bank[0]
        p_dw = bank[7][:, 0:NT * WS * BLOCK]
        p_s, p_pt, p_or = [bank[2], bank[3]], [bank[6], bank[7]], [bank[0], bank[5]]

        def p_k(j, q):
            return bank[5] if j == 0 and q % 2 else bank[4]

        p_rj = p_ix[:, 0:P]
        p_br = p_ix[0:NR, 128:128 + NRT]
        p_cw = p_ix[:, 132:132 + BLOCK]
        p_ct = p_ix[:, 160:160 + NRT * BLOCK]
        p_keep = p_ix[:, 256:256 + NRT * BLOCK]

        s_rm = sem("s_rm"); s_tab = sem("s_tab"); s_c0 = sem("s_c0"); s_c1 = sem("s_c1"); s_c2 = sem("s_c2")
        s_x = sem("s_x"); s_w = sem("s_w"); s_wo = sem("s_wo"); s_scl = sem("s_scl"); s_sel = sem("s_sel")
        s_dve = sem("s_dve"); s_sh = sem("s_sh")
        s_ci = sem("s_ci")
        s_mvr = sem("s_mvr"); s_mvj = sem("s_mvj")
        s_br = sem("s_br"); s_ix = sem("s_ix"); s_rr = sem("s_rr")
        s_gi = sem("s_gi")
        s_nri = sem("s_nri"); s_mat = sem("s_mat"); s_cnt = sem("s_cnt"); s_ovr = sem("s_ovr"); s_cw = sem("s_cw"); s_dc = sem("s_dc"); s_dw = sem("s_dw"); s_dst = sem("s_dst")
        s_mc = sem("s_mc"); s_msq = sem("s_msq"); s_msk = sem("s_msk")
        s_ang = sem("s_ang"); s_trig = sem("s_trig")
        s_zero = sem("s_zero"); s_zr1 = sem("s_zr1"); s_init = sem("s_init")
        s_wg = [sem(f"s_wg{i}") for i in range(NT)]
        s_k = [sem(f"s_k{i}") for i in range(NRT)]
        s_v = [sem(f"s_v{i}") for i in range(NRT)]
        s_n = [sem(f"s_n{i}") for i in range(NRT)]
        s_sc = sem("s_sc")
        s_wbd = sem("s_wbd"); s_pxr = sem("s_pxr"); s_x1 = sem("s_x1"); s_pxt = sem("s_pxt"); s_xt = sem("s_xt")
        s_pkv = sem("s_pkv"); s_vc = sem("s_vc"); s_ksum = sem("s_ksum"); s_kread = sem("s_kread")
        s_krt = sem("s_krt"); s_new = sem("s_new")
        s_pq = sem("s_pq"); s_qsq = sem("s_qsq"); s_qsum = sem("s_qsum"); s_qrt = sem("s_qrt"); s_rot = sem("s_rot")
        s_qread = sem("s_qread")
        s_pqt = sem("s_pqt"); s_qz = sem("s_qz"); s_qbd = sem("s_qbd")
        s_mv_ = sem("s_mrg_v"); s_mk = sem("s_mrg_k"); s_vst = sem("s_vst")
        s_vs = [sem(f"s_vs{i}") for i in range(NRT)]
        s_pk = sem("s_pk"); s_kt = sem("s_kt")
        s_ps = sem("s_ps"); s_nmx = sem("s_nmx"); s_pr = sem("s_pr"); s_ppt = sem("s_ppt"); s_pts = sem("s_pts")
        s_am = sem("s_am"); s_po = sem("s_po"); s_r = sem("s_r"); s_ot = sem("s_ot"); s_py = sem("s_py")
        s_y = sem("s_y"); s_out = [sem("s_out0"), sem("s_out1")]

        block = ctx.enter_context(nc.Block())

        @block.sync
        def _(sp):
            sp.dma_start(rm_i[:], row_meta).then_inc(s_rm, 16)
            sp.dma_start(cst[:, 0:NFIRST], consts[:, 0:NFIRST]).then_inc(s_c0, 16)
            sp.dma_start(tab_i[:], tables).then_inc(s_tab, 16)
            sp.dma_start(cst[:, NFIRST:NEARLY], consts[:, NFIRST:NEARLY]).then_inc(s_c1, 16)
            sp.dma_start(xs[:], x.rearrange("(n b) t d -> (b t) n d", b=BB)).then_inc(s_x, 16)
            sp.dma_start(cst[:, NEARLY:], consts[:, NEARLY:]).then_inc(s_c2, 16)
            sp.dma_start(w_sb[:], w_all.rearrange("(h p) n -> p h n", p=P)).then_inc(s_w, 16)
            sp.dma_start(scl[:], scales.rearrange("p (a b) -> p a b", a=2)).then_inc(s_scl, 16)
            sp.dma_start(selb[:].rearrange("p a b -> p (a b)"), sel).then_inc(s_sel, 16)
            sp.dma_start(wo_sb[:], wo_t.rearrange("(h p) n -> p h n", p=P)).then_inc(s_wo, 16)
            sp.wait_ge(s_zero, 1)
            sp.wait_ge(s_wg[NT - 1], 16)
            sp.dma_start(new_tab.rearrange("(j o) f -> j (o f)", o=BLOCK),
                         mrg[0:NJ, 0, :, :].rearrange("p o f -> p (o f)")).then_inc(s_init, 16)
            for j in range(NRT):
                n = RB_[j] * NS
                sp.wait_ge(s_mv_, j + 1)
                sp.dma_start(v_tab[R0[j] * SP_:(R0[j] + RB_[j]) * SP_, :].rearrange("(r o) f -> r o f", o=BLOCK),
                             mrg[0:n, j % 2, :, GD:]).then_inc(s_vst, 16)
                sp.wait_ge(s_vst, 16 * (j + 1))
                if j >= 2:
                    sp.wait_ge(s_po, R0[j - 1])
                sp.dma_start(vs[:, V0[j]:V0[j] + 2 * RB_[j], :],
                             v_tab[R0[j] * SP_:(R0[j] + RB_[j]) * SP_, :].rearrange("(r p) f -> p r f", p=HS)
                             ).then_inc(s_vs[j], 16)
            out_v = out.rearrange("(n b) t d -> n (b t) d", b=BB)
            for n in range(NT):
                sp.wait_ge(s_y, n + 1)
                sp.dma_start(out_v[n], yo[:, n % 2, :]).then_inc(s_out[n % 2], 16)
            for i in range(2):
                sp.wait_ge(s_out[i], 16 * (NT // 2))

        @block.gpsimd
        def _(pool):
            nc.gpsimd.memset(mrg[:, 0], 0.0).then_inc(s_zero, 1)
            pool.wait_ge(s_ci, 1)
            for n in range(NT):
                pool.indirect_dma_start(wg[:, n, :], None, w0, bass.IndirectOffsetOnAxis(ap=cond_i[:, n:n + 1], axis=0),
                                        bounds_check=200 * T - 1, oob_is_err=False).then_inc(s_wg[n], 16)

            def gather_old(dst, src, j, s):
                n = RB_[j] * NS
                pool.indirect_dma_start(dst[0:n, j % 2, :], None, src.rearrange("n g o d -> n (g o d)"),
                                        bass.IndirectOffsetOnAxis(ap=blk_ri[0:n, j:j + 1], axis=0),
                                        bounds_check=NPOOL - 1, oob_is_err=False).then_inc(s, 16)

            pool.wait_ge(s_gi, 1)
            for j in range(2):
                gather_old(v_old, vb, j, s_v[j])
                gather_old(k_old, kb, j, s_k[j])
            nc.gpsimd.memset(mrg[:, 1], 0.0).then_inc(s_zr1, 1)

            def window(n):
                pool.wait_ge(s_msq, n + 1)
                nc.gpsimd.tensor_scalar(mask[:, n, :], sq_m[:, n % 2, :], 64.0 * 64.0, NEG, ALU.is_gt, ALU.mult
                                        ).then_inc(s_msk, 1)

            window(0)
            window(1)
            pool.wait_ge(s_dst, 1)
            pool.wait_ge(s_init, 16)
            for n in range(NT):
                if n % 2 == 0:
                    window(2 + n // 2)
                    pool.wait_ge(s_new, n // 2 + 1)
                    pool.wait_ge(s_vc, n // 2 + 1)
                pool.indirect_dma_start(new_tab, bass.IndirectOffsetOnAxis(ap=dst_i[:, n:n + 1], axis=0),
                                        new[:, n, :], None,
                                        bounds_check=NJ * BLOCK - 1, oob_is_err=False).then_inc(s_sc, 16)
            pool.wait_ge(s_sc, 16 * NT)
            pool.wait_ge(s_nri, 1)
            pool.wait_ge(s_zr1, 1)
            for j in range(NRT):
                n = RB_[j] * NS
                if j >= 2:
                    pool.wait_ge(s_pk, 4 * (j - 1))
                    pool.wait_ge(s_vst, 16 * (j - 1))
                pool.indirect_dma_start(mrg[0:n, j % 2, :, :].rearrange("p o f -> p (o f)"), None,
                                        new_tab.rearrange("(j o) f -> j (o f)", o=BLOCK),
                                        bass.IndirectOffsetOnAxis(ap=new_ri[0:n, j:j + 1], axis=0),
                                        bounds_check=NJ - 1, oob_is_err=False).then_inc(s_n[j], 16)
                if j == 1:
                    pool.wait_ge(s_mv_, 1)
                    gather_old(v_old, vb, 2, s_v[2])
                    pool.wait_ge(s_mk, 1)
                    gather_old(k_old, kb, 2, s_k[2])
            window(6)
            window(7)

        @block.vector
        def _(dve):
            steps = [0]
            V = nc.vector

            def link(ins):
                steps[0] += 1
                ins.then_inc(s_dve, 1)
                dve.wait_ge(s_dve, steps[0])

            V.memset(mv_r[:, B, :], 0.0)
            dve.wait_ge(s_rm, 16)
            link(V.tensor_copy(rm[:], rm_i[:]))
            dve.wait_ge(s_c0, 16)
            V.tensor_scalar(wq8[:, 1, :], kv_w, const("tcol"), None, ALU.add)
            link(V.tensor_scalar(wq8[:, 0, :], cond_w, float(T), const("tcol"), ALU.mult, ALU.add))
            V.tensor_copy(cond_i[:], wq8[:, 0, :]).then_inc(s_ci, 1)
            V.tensor_scalar(fl[:, 0:NT], kv_w, 1.0 / BLOCK, -(WINDOW - 1) / BLOCK - 15 / 32, ALU.mult, ALU.add)
            V.tensor_scalar(fl[:, NT:2 * NT], kv_w, 1.0 / BLOCK, -15 / 32, ALU.mult, ALU.add)
            V.tensor_scalar(fl[:, 2 * NT:3 * NT], wq8[:, 1, :], 1.0 / BLOCK, -15 / 32, ALU.mult, ALU.add)
            V.tensor_scalar(fl[:, 3 * NT:3 * NT + 1], kv, 1.0 / BLOCK, -(WINDOW - 1) / BLOCK - 15 / 32, ALU.mult, ALU.add)
            link(V.tensor_scalar(fl[:, 3 * NT + 1:], kv, 1.0 / BLOCK, -15 / 32, ALU.mult, ALU.add))
            link(V.tensor_scalar(fl[:], fl[:], MAGIC, None, ALU.add))
            link(V.tensor_scalar(fl[:], fl[:], MAGIC, None, ALU.subtract))
            V.tensor_scalar(fl[:, 0:NT], fl[:, 0:NT], 0.0, None, ALU.max)
            link(V.tensor_scalar(fl[:, 3 * NT:3 * NT + 1], fl[:, 3 * NT:3 * NT + 1], 0.0, None, ALU.max))
            V.tensor_scalar(base[:, 0:3], const("slot_of")[:, 0:3], fl[:, 3 * NT:3 * NT + 1], None, ALU.add)
            V.tensor_scalar(base[:, 3:4], const("slot_of")[:, 3:4], fl[:, 3 * NT + 1:], None, ALU.add)
            dve.wait_ge(s_tab, 16)
            link(V.tensor_copy(tab[:], tab_i[:]))
            for i in range(4):
                last = V.scalar_tensor_tensor(out=scratch[:, i * NBLK:(i + 1) * NBLK], in0=const("iota"),
                                              scalar=base[:, i:i + 1], in1=tab[:],
                                              op0=ALU.is_equal, op1=ALU.mult, accum_out=found[:, i:i + 1])
            link(last)
            dve.wait_ge(s_c1, 16)
            pick_r = const("pick_r").rearrange("p (b s) -> p b s", s=NS)
            V.tensor_tensor(mv_r[:, 0:B, 0:2 * KK].rearrange("p b (i k) -> p b i k", k=KK),
                            pick_r[:, :, 0:2 * KK].rearrange("p b (i k) -> p b i k", k=KK),
                            found[:, 0:2].unsqueeze(1).unsqueeze(3).broadcast_to([P, B, 2, KK]), ALU.mult)
            V.tensor_tensor(mv_r[:, 0:B, 2 * KK:NS], pick_r[:, :, 2 * KK:NS],
                            found[:, 2:3].unsqueeze(2).broadcast_to([P, B, NS - 2 * KK]), ALU.mult).then_inc(s_mvr, 1)
            V.tensor_scalar(mv_j[:], ident, found[:, 3:4], None, ALU.mult).then_inc(s_mvj, 1)
            dve.wait_ge(s_br, 1)
            V.tensor_copy(blk_rf[:], p_br)
            V.tensor_copy(blk_ri[:], p_br).then_inc(s_gi, 1)
            dve.wait_ge(s_c2, 16)
            link(V.tensor_tensor(ang[:], wq8[:, 1, :].unsqueeze(2).broadcast_to([P, NT, HD // 2]),
                                 const("invf").unsqueeze(1).broadcast_to([P, NT, HD // 2]), ALU.mult))
            link(V.tensor_scalar(turn[:], ang[:], 1.0 / (2 * np.pi), MAGIC, ALU.mult, ALU.add))
            link(V.tensor_scalar(turn[:], turn[:], MAGIC, None, ALU.subtract))
            for c in (C1, C2, C3):
                link(V.scalar_tensor_tensor(out=ang[:], in0=turn[:], scalar=-c, in1=ang[:], op0=ALU.mult, op1=ALU.add))
            V.tensor_scalar(ang[:], ang[:], PI_, -PI_, ALU.min, ALU.max).then_inc(s_ang, 1)
            V.scalar_tensor_tensor(out=mask_c[:], in0=fl[:, 0:NT], scalar=float(BLOCK), in1=kv_w,
                                   op0=ALU.mult, op1=ALU.subtract).then_inc(s_mc, 1)
            dve.wait_ge(s_scl, 16)
            link(V.tensor_scalar(ga[:], scl[:], 1.0, None, ALU.add))
            link(V.tensor_scalar(ga[:, 0, :], ga[:, 0, :], SCALE, None, ALU.mult))
            V.tensor_copy(gb[:, :, 16:32], ga[:, :, 0:16])
            link(V.tensor_scalar(gb[:, :, 0:16], ga[:, :, 16:32], -1.0, None, ALU.mult))

            link(V.scalar_tensor_tensor(out=ix[:, 2:3], in0=base[:, 3:4], scalar=-float(BLOCK), in1=kv,
                                        op0=ALU.mult, op1=ALU.add))
            V.tensor_scalar(cov_a[:, 0, :], const("off16"), ix[:, 2:3], None, ALU.subtract)
            link(V.tensor_scalar(cov_a[:, 1, :], const("off16"), ix[:, 2:3], None, ALU.subtract))
            link(V.tensor_scalar(cov_a[:, 0, :], cov_a[:, 0, :], 0.0, None, ALU.is_ge))
            link(V.tensor_scalar(cov_a[:, 1, :], cov_a[:, 1, :], float(T), None, ALU.is_lt))
            link(V.tensor_tensor(cover[:], cov_a[:, 0, :], cov_a[:, 1, :], ALU.mult))

            def tables_of_rotation():
                dve.wait_ge(s_trig, 1)
                link(V.tensor_scalar(cos_[:], cos_[:], -2.0, 1.0, ALU.mult, ALU.add))
                for a in (1, 0):
                    for tt, gg, tr in ((t1, ga, cos_), (t2, gb, sin_)):
                        last = V.tensor_tensor(tt[:, a].rearrange("p n (h i) -> p n h i", h=2),
                                               gg[:, a].rearrange("p (h i) -> p h i", h=2).unsqueeze(1).broadcast_to([P, NT, 2, 16]),
                                               tr[:].unsqueeze(2).broadcast_to([P, NT, 2, 16]), ALU.mult)
                link(last)

            def wbd_tile(n):
                dve.wait_ge(s_wg[n], 16)
                V.tensor_tensor(wbd[:, n], wg[:, n, :].unsqueeze(1).broadcast_to([P, BB, T]),
                                const("bd").unsqueeze(2).broadcast_to([P, BB, T]), ALU.mult).then_inc(s_wbd, 1)

            def rotate(px, a, n, heads, s_sum, count, s_read, s_root):
                f = 2 * heads * HD
                av = ra[:, 0:f].rearrange("p (k h d) -> p k h d", k=2, d=HD)
                bv = rb[:, 0:f].rearrange("p (k h d) -> p k h d", k=2, d=HD)
                V.tensor_reduce(ms[:, 0:2 * heads], sq[:, 0:f].rearrange("p (h d) -> p h d", d=HD), AX_X,
                                ALU.add).then_inc(s_sum, 1)
                V.tensor_tensor(av, px, t1[:, a, n:n + 2, :].unsqueeze(2).broadcast_to([P, 2, heads, HD]), ALU.mult)
                V.tensor_tensor(bv[:, :, :, 0:16], px[:, :, :, 16:32],
                                t2[:, a, n:n + 2, 0:16].unsqueeze(2).broadcast_to([P, 2, heads, 16]), ALU.mult)
                V.tensor_tensor(bv[:, :, :, 16:32], px[:, :, :, 0:16],
                                t2[:, a, n:n + 2, 16:32].unsqueeze(2).broadcast_to([P, 2, heads, 16]), ALU.mult).then_inc(s_read, 1)
                dve.wait_ge(s_read, count)
                V.tensor_tensor(ra[:, 0:f], ra[:, 0:f], rb[:, 0:f], ALU.add)
                dve.wait_ge(s_root, count)
                link(V.reciprocal(rstd[:, 0:2 * heads], rt[:, 0:2 * heads]))
                return av, rstd[:, 0:2 * heads].rearrange("p (k h) -> p k h", k=2).unsqueeze(3).broadcast_to([P, 2, heads, HD])

            def keys_pair(i):
                if i >= 1:
                    dve.wait_ge(s_new, i)
                dve.wait_ge(s_vc, i + 1)
                av, rs = rotate(p_kv[i % 2][:].rearrange("p (k c h d) -> p k c h d", k=2, c=2, d=HD)[:, :, 0], 1, 2 * i, G,
                                s_ksum, i + 1, s_kread, s_krt)
                V.tensor_tensor(new[:, 2 * i:2 * i + 2, 0:GD].rearrange("p k (h d) -> p k h d", d=HD), av, rs,
                                ALU.mult).then_inc(s_new, 1)

            def queries_pair(i):
                if i == 0:
                    dve.wait_ge(s_new, NP_)
                else:
                    dve.wait_ge(s_rot, i)
                dve.wait_ge(s_qsq, i + 1)
                if i >= 2:
                    dve.wait_ge(s_pqt, i - 1)
                av, rs = rotate(p_q[i % 2][:].rearrange("p (k h d) -> p k h d", k=2, d=HD), 0, 2 * i, H,
                                s_qsum, i + 1, s_qread, s_qrt)
                V.tensor_tensor(rq[:, i % 2, :].rearrange("p (k h d) -> p k h d", k=2, d=HD), av, rs, ALU.mult).then_inc(s_rot, 1)

            def over_index():
                dve.wait_ge(s_ix, 1)
                link(V.tensor_copy(rows_j[:], p_rj))
                V.scalar_tensor_tensor(out=over[:], in0=rows_j[:], scalar=found[:, 3:4], in1=const("later"),
                                       op0=ALU.is_equal, op1=ALU.mult).then_inc(s_ovr, 1)
                link(V.scalar_tensor_tensor(out=dwork[:, 0:P], in0=rows_j[:], scalar=found[:, 3:4], in1=const("order"),
                                            op0=ALU.is_equal, op1=ALU.mult))
                link(V.tensor_reduce(dcol[:, 0:1], dwork[:, 0:P], AX_X, ALU.max))
                link(V.tensor_scalar(dcol[:, 1:2], dcol[:, 0:1], float(BLOCK), -float(BLOCK), ALU.mult, ALU.add))
                link(V.tensor_scalar(dcell[:, 0, :], const("off16"), dcol[:, 1:2], None, ALU.add))
                link(V.scalar_tensor_tensor(out=wq8[:, 2, :], in0=fl[:, NT:2 * NT], scalar=-float(BLOCK), in1=wq8[:, 1, :],
                                            op0=ALU.mult, op1=ALU.add))
                V.tensor_tensor(here, const("cell").unsqueeze(1).broadcast_to([P, NT, WS * BLOCK]),
                                wq8[:, 2, :].unsqueeze(2).broadcast_to([P, NT, WS * BLOCK]), ALU.is_equal)
                dve.wait_ge(s_cw, 1)
                link(V.scalar_tensor_tensor(out=dcell[:, 1, :], in0=p_cw, scalar=BIG, in1=dcell[:, 0, :],
                                            op0=ALU.mult, op1=ALU.add))
                V.tensor_tensor(dwork.rearrange("p (v o) -> p v o", o=BLOCK),
                                const("pick_w").unsqueeze(2).broadcast_to([P, NT * WS, BLOCK]),
                                dcell[:, 1, :].unsqueeze(1).broadcast_to([P, NT * WS, BLOCK]), ALU.mult).then_inc(s_dc, 1)

            def rows_index():
                dve.wait_ge(s_dw, 1)
                link(V.tensor_tensor(dpick, here.rearrange("p n c -> p (n c)"), p_dw, ALU.mult))
                link(V.tensor_reduce(wq8[:, 3, :], dpick.rearrange("p (n c) -> p n c", c=WS * BLOCK), AX_X, ALU.add))
                V.tensor_copy(dst_i[:], wq8[:, 3, :]).then_inc(s_dst, 1)

            def match_index():
                dve.wait_ge(s_rr, 1)
                V.tensor_scalar(match[:], p_rr.rearrange("p (b s) -> p b s", s=NS), found[:, 3:4], None, ALU.is_equal
                                ).then_inc(s_mat, 1)

            def readers_index():
                link(V.tensor_tensor(rwork[0:NR], rows_j[0:NR].unsqueeze(1).broadcast_to([NR, NRT, P]),
                                     blk_rf[:].unsqueeze(2).broadcast_to([NR, NRT, P]), ALU.is_equal))
                link(V.tensor_tensor(rwork[0:NR], rwork[0:NR],
                                     const("order")[0:NR].unsqueeze(1).broadcast_to([NR, NRT, P]), ALU.mult))
                link(V.tensor_reduce(cnt_rf[:], rwork[0:NR], AX_X, ALU.max))
                link(V.tensor_scalar(blk_rf[:], cnt_rf[:], 0.0, BIG, ALU.is_equal, ALU.mult))
                link(V.scalar_tensor_tensor(out=blk_rf[:], in0=cnt_rf[:], scalar=-1.0, in1=blk_rf[:],
                                            op0=ALU.add, op1=ALU.add))
                V.tensor_copy(new_ri[:], blk_rf[:]).then_inc(s_nri, 1)

            def keep_masks():
                dve.wait_ge(s_cnt, 1)
                for j in range(NRT):
                    n = RB_[j] * NS
                    last = V.tensor_scalar(p_keep[0:n, j * BLOCK:(j + 1) * BLOCK].bitcast(I32),
                                           p_ct[0:n, j * BLOCK:(j + 1) * BLOCK], 0.0, None, ALU.is_equal)
                link(last)

            for n in range(4):
                wbd_tile(n)
            match_index()
            over_index()
            tables_of_rotation()
            for n in range(4, NT):
                wbd_tile(n)
            rows_index()
            for i in range(NP_):
                keys_pair(i)
                if i == 0:
                    readers_index()
                if i == 1:
                    keep_masks()
            for i in range(NP_):
                queries_pair(i)

            def merge(j, old, s_old, f0, s_done):
                n = RB_[j] * NS
                dve.wait_ge(s_old, 16)
                dve.wait_ge(s_n[j], 16)
                dst = mrg[0:n, j % 2, :, f0:f0 + GD].rearrange("p o (g d) -> p o g d", d=HD)
                keep = p_keep[0:n, j * BLOCK:(j + 1) * BLOCK].bitcast(I32).unsqueeze(2).unsqueeze(3).broadcast_to([n, BLOCK, G, HD])
                V.copy_predicated(dst, keep, old[0:n, j % 2, :].rearrange("p (g o d) -> p o g d", g=G, d=HD)).then_inc(s_done, 1)

            def rows_out(n):
                dve.wait_ge(s_py, n + 1)
                if n >= 2:
                    dve.wait_ge(s_out[n % 2], 16 * (n // 2))
                V.tensor_tensor(yo[:, n % 2, :], p_or[n % 2][:, 0:D], x1[:, n, :], ALU.add).then_inc(s_y, 1)

            for b in range(B + 4):
                if b in MERGE_V:
                    j = MERGE_V.index(b)
                    merge(j, v_old, s_v[j], GD, s_mv_)
                if b in MERGE_K:
                    j = MERGE_K.index(b)
                    merge(j, k_old, s_k[j], 0, s_mk)
                if b < B:
                    dve.wait_ge(s_ps, b + 1)
                    if b >= 3:
                        dve.wait_ge(s_pr, 2 * (b - 2))
                    V.tensor_reduce(nmx[:, b % 3, :], p_s[b % 2][:, 0:2 * SP_].rearrange("p (a s) -> p a s", a=2), AX_X,
                                    ALU.max, negate=True).then_inc(s_nmx, 1)
                c = b - 1
                if 0 <= c < B:
                    dve.wait_ge(s_pr, 2 * c + 2)
                    link(V.reciprocal(rin[:, c % 3, :], sums[:, c % 3, :]))
                    if c >= 2:
                        dve.wait_ge(s_po, c - 1)
                    V.tensor_tensor(amat[:, c % 2, :].rearrange("p (a f) -> p a f", a=2),
                                    const("gmask").rearrange("p (a f) -> p a f", a=2),
                                    rin[:, c % 3, :].unsqueeze(2).broadcast_to([P, 2, 64]), ALU.mult).then_inc(s_am, 1)
                k = (b - BB - 2) // BB
                if b >= BB + 2 and b % BB == 2 and k < NT:
                    dve.wait_ge(s_r, k + 1)
                    if k >= 2:
                        dve.wait_ge(s_py, k - 1)
                    V.tensor_tensor(ot[:, :, k % 2].rearrange("p h b t -> p b h t"),
                                    p_or[k % 2][:, 0:256].rearrange("p (b h t) -> p b h t", b=BB, h=HH),
                                    r_sb[:, k % 2, :].rearrange("p (b h t) -> p b h t", b=BB, h=HH), ALU.mult).then_inc(s_ot, 1)
                if b >= 2 * BB and b % BB == 0:
                    rows_out(b // BB - 2)
            rows_out(NT - 1)

        @block.scalar
        def _(act):
            A = nc.scalar

            A.memzero(qbd[:].rearrange("p b a f -> p (b a f)")).then_inc(s_qz, 1)
            act.wait_ge(s_ang, 1)
            A.activation(sin_[:], ang[:], ACT.Sin)
            A.activation(cos_[:], ang[:], ACT.Sin, scale=0.5).then_inc(s_sh, 1)
            act.wait_ge(s_sh, 1)
            A.activation(cos_[:], cos_[:], ACT.Square).then_inc(s_trig, 1)

            def window(n):
                if n == 0:
                    act.wait_ge(s_mc, 1)
                if n >= 2:
                    act.wait_ge(s_msk, n - 1)
                A.activation(sq_m[:, n % 2, :], const("jrow"), ACT.Square, bias=mask_c[:, n:n + 1]).then_inc(s_msq, 1)

            window(0)
            window(1)
            for i in range(NP_ + 1):
                if i < NP_:
                    act.wait_ge(s_pxt, i + 1)
                    A.activation(xt[:, 2 * i:2 * i + 2].rearrange("p k h f -> p (k h f)"), p_xt[i % 2][:], ACT.Copy).then_inc(s_xt, 1)
                    window(2 + i)
                n = i - 1
                if 0 <= n:
                    act.wait_ge(s_pkv, n + 1)
                    if n >= 1:
                        act.wait_ge(s_ksum, n)
                    kv_ = p_kv[n % 2][:].rearrange("p (k c) -> p k c", k=2)
                    A.activation(sq[:, 0:2 * GD].rearrange("p (k c) -> p k c", k=2), kv_[:, :, 0:GD], ACT.Square)
                    A.activation(new[:, 2 * n:2 * n + 2, GD:], kv_[:, :, GD:], ACT.Copy).then_inc(s_vc, 1)
                    act.wait_ge(s_ksum, n + 1)
                    if n >= 1:
                        act.wait_ge(s_new, n)
                    A.activation(rt[:, 0:2 * G], ms[:, 0:2 * G], ACT.Sqrt, scale=1.0 / HD, bias=const("eps")).then_inc(s_krt, 1)

            for i in range(NP_ + 1):
                if i < NP_:
                    act.wait_ge(s_pq, i + 1)
                    if i >= 1:
                        act.wait_ge(s_qsum, i)
                    A.activation(sq[:], p_q[i % 2][:], ACT.Square).then_inc(s_qsq, 1)
                    act.wait_ge(s_pxr, i + 1)
                    A.activation(x1[:, 2 * i:2 * i + 2, :].rearrange("p k f -> p (k f)"), p_xr[:], ACT.Copy).then_inc(s_x1, 1)
                    act.wait_ge(s_qsum, i + 1)
                    if i == 0:
                        act.wait_ge(s_new, NP_)
                    else:
                        act.wait_ge(s_rot, i)
                    A.activation(rt[:, 0:2 * H], ms[:, 0:2 * H], ACT.Sqrt, scale=1.0 / HD, bias=const("eps")).then_inc(s_qrt, 1)
                n = i - 1
                if 0 <= n:
                    act.wait_ge(s_pqt, n + 1)
                    if n == 0:
                        act.wait_ge(s_qz, 1)
                    for n in (2 * i - 2, 2 * i - 1):
                        for g in range(G):
                            last = A.activation(
                                qbd[HD * g:HD * (g + 1), BB * n:BB * (n + 1), g // 2, (g % 2) * 64:(g % 2) * 64 + 64
                                    ].rearrange("p b (h t) -> p b h t", h=HH),
                                p_qt[(n // 2) % 2][HD * g:HD * (g + 1), (n % 2) * HH * P:(n % 2 + 1) * HH * P
                                                   ].rearrange("p (h b t) -> p b h t", h=HH, b=BB), ACT.Copy)
                    last.then_inc(s_qbd, 1)
            window(6)
            window(7)

            def keys(j, q):
                n = RB_[j] * NS
                if j >= 2:
                    act.wait_ge(s_ps, R0[j - 1])
                act.wait_ge(s_pk, 4 * j + q + 1)
                A.activation(kt[:, K0[j]:K0[j] + RB_[j] * SP_].rearrange("p (r o) -> p r o", o=BLOCK)[:, :, 4 * q:4 * q + 4],
                             p_k(j, q)[:, 0:4 * n].rearrange("p (o r) -> p r o", o=4), ACT.Copy).then_inc(s_kt, 1)

            for q in range(4):
                keys(0, q)
            for b in range(B + 4):
                if b in KEYS_AT:
                    keys(*KEYS_AT[b])
                c = b - 1
                if 0 <= c < B:
                    act.wait_ge(s_ppt, c + 1)
                    if c >= 2:
                        act.wait_ge(s_po, c - 1)
                    A.activation(pts[:, c % 2].rearrange("p a b f -> p (a b f)"), p_pt[c % 2][0:HS, :], ACT.Copy
                                 ).then_inc(s_pts, 1)
                if b < B:
                    act.wait_ge(s_nmx, b + 1)
                    if b >= 3:
                        act.wait_ge(s_ppt, b - 2)
                        act.wait_ge(s_am, b - 2)
                    for a in range(2):
                        A.activation(pr[:, b % 3, a, :], p_s[b % 2][:, a * SP_:(a + 1) * SP_], ACT.Exp,
                                     bias=nmx[:, b % 3, a:a + 1], accum_out=sums[:, b % 3, a:a + 1]).then_inc(s_pr, 1)
                k = (b - BB - 2) // BB
                if b >= BB + 2 and b % BB == 2 and k < NT:
                    act.wait_ge(s_po, BB * (k + 1))
                    if k >= 2:
                        act.wait_ge(s_ot, k - 1)
                    A.activation(r_sb[:, k % 2, :], p_or[k % 2][:, 256:512], ACT.Copy).then_inc(s_r, 1)

        @block.tensor
        def _(pe):
            mm = pe.matmul
            pe.wait_ge(s_c1, 16)
            pe.wait_ge(s_mvr, 1)
            for j in range(NRT):
                last = mm(p_br[:, j:j + 1], mv_r[:, R0[j]:R0[j] + RB_[0], :].rearrange("p b s -> p (b s)"), ones[:, 0:1],
                          start=True, stop=True)
            last.then_inc(s_br, 1)
            pe.wait_ge(s_mvj, 1)
            pe.wait_ge(s_gi, 1)
            mm(p_rj, ones, mv_j[:], start=True, stop=True).then_inc(s_ix, 1)
            mm(p_rr, ones, mv_r[:, 0:B, :].rearrange("p b s -> p (b s)"), start=True, stop=True).then_inc(s_rr, 1)

            def x1_pair(i):
                pe.wait_ge(s_wbd, 2 * i + 2)
                if i >= 2:
                    pe.wait_ge(s_xt, i - 1)
                for n in (2 * i, 2 * i + 1):
                    for h in range(2):
                        o = p_xt[i % 2][:, (2 * (n % 2) + h) * P:(2 * (n % 2) + h + 1) * P]
                        mm(o, xs[:, n, h * P:(h + 1) * P], ident, start=True, stop=False)
                        last = mm(o, xs[:, n, h * P:(h + 1) * P], wbd[:, n].rearrange("p b t -> p (b t)"), start=False, stop=True)
                last.then_inc(s_pxt, 1)

            def project(o, n, c0, c1):
                for h in range(2):
                    last = mm(o, xt[:, n, h, :], w_sb[:, h, c0:c1], start=(h == 0), stop=(h == 1))
                return last

            def keys_values(i):
                pe.wait_ge(s_xt, i + 1)
                if i == 0:
                    pe.wait_ge(s_w, 16)
                if i >= 2:
                    pe.wait_ge(s_kread, i - 1)
                for k in range(2):
                    last = project(p_kv[i % 2][:, k * 2 * GD:(k + 1) * 2 * GD], 2 * i + k, H * HD, NW)
                last.then_inc(s_pkv, 1)

            def queries(i):
                if i == 0:
                    pe.wait_ge(s_xt, NP_)
                if i >= 2:
                    pe.wait_ge(s_qread, i - 1)
                for k in range(2):
                    last = project(p_q[i % 2][:, k * H * HD:(k + 1) * H * HD], 2 * i + k, 0, H * HD)
                last.then_inc(s_pq, 1)

            def x1_rows(i):
                if i >= 1:
                    pe.wait_ge(s_x1, i)
                for k in range(2):
                    for h in range(2):
                        last = pe.transpose(p_xr[:, (2 * k + h) * P:(2 * k + h + 1) * P], xt[:, 2 * i + k, h, :], ident)
                last.then_inc(s_pxr, 1)

            def queries_turn(i):
                pe.wait_ge(s_rot, i + 1)
                if i >= 2:
                    pe.wait_ge(s_qbd, i - 1)
                for c in range(2 * HH):
                    last = pe.transpose(p_qt[i % 2][:, c * P:(c + 1) * P], rq[:, i % 2, c * P:(c + 1) * P], ident)
                last.then_inc(s_pqt, 1)

            pe.wait_ge(s_x, 16)
            x1_pair(0)
            pe.wait_ge(s_ovr, 1)
            mm(p_cw, over[:], cover[:], start=True, stop=True).then_inc(s_cw, 1)
            x1_pair(1)
            keys_values(0)
            pe.wait_ge(s_mat, 1)
            pe.wait_ge(s_dc, 1)
            mm(p_dw, const("row_of"), dwork, start=True, stop=True).then_inc(s_dw, 1)
            for j in range(NRT):
                last = mm(p_ct[0:RB_[j] * NS, j * BLOCK:(j + 1) * BLOCK],
                          match[:, R0[j]:R0[j] + RB_[j], :].rearrange("p b s -> p (b s)"), cover[:],
                          start=True, stop=True)
            last.then_inc(s_cnt, 1)
            x1_pair(2)
            keys_values(1)
            x1_pair(3)
            keys_values(2)
            keys_values(3)
            queries(0)
            x1_rows(0)
            queries(1)
            for i in range(NP_):
                queries_turn(i)
                if i + 1 < NP_:
                    x1_rows(i + 1)
                if i + 2 < NP_:
                    queries(i + 2)

            def keys(j, q):
                n = RB_[j] * NS
                pe.wait_ge(s_mk, j + 1)
                if j == 0 and q >= 2:
                    pe.wait_ge(s_kt, q - 1)
                for o in range(4):
                    last = pe.transpose(p_k(j, q)[:, o * n:(o + 1) * n], mrg[0:n, j % 2, 4 * q + o, 0:GD], ident[0:n, 0:n])
                last.then_inc(s_pk, 1)

            pe.wait_ge(s_kread, NP_)
            for q in range(4):
                keys(0, q)
            for b in range(B + 4):
                if b in KEYS_AT:
                    pe.wait_ge(s_kt, 4 + sum(a < b for a in KEYS_AT))
                    keys(*KEYS_AT[b])
                if b < B:
                    if b == 0:
                        pe.wait_ge(s_sel, 16)
                    if b % BB == 0:
                        pe.wait_ge(s_msk, b // BB + 1)
                    if b == 0:
                        pe.wait_ge(s_qbd, NP_)
                        pe.wait_ge(s_x1, NP_)
                    if b in R0:
                        pe.wait_ge(s_kt, 4 * (R0.index(b) + 1))
                    if b >= 2:
                        pe.wait_ge(s_pr, 2 * (b - 1))
                    tj = b // RB_[0]
                    k0 = K0[tj] + (b - R0[tj]) * SP_
                    for a in range(2):
                        o = p_s[b % 2][:, a * SP_:(a + 1) * SP_]
                        mm(o, qbd[:, b, a, :], kt[:, k0:k0 + SP_], start=True, stop=False)
                        last = mm(o, selb[:, b % BB, :], mask[:, b // BB, :], start=False, stop=True)
                    last.then_inc(s_ps, 1)
                c = b - 1
                if 0 <= c < B:
                    pe.wait_ge(s_pr, 2 * c + 2)
                    if c >= 2:
                        pe.wait_ge(s_pts, c - 1)
                    for hf in range(2):
                        for a in range(2):
                            k = 2 * hf + a
                            last = pe.transpose(p_pt[c % 2][0:HS, k * P:(k + 1) * P], pr[:, c % 3, a, hf * HS:(hf + 1) * HS], ident)
                    last.then_inc(s_ppt, 1)
                e = b - 2
                if 0 <= e < B:
                    pe.wait_ge(s_pts, e + 1)
                    pe.wait_ge(s_am, e + 1)
                    if e in R0:
                        pe.wait_ge(s_vs[R0.index(e)], 16)
                    k = e // BB
                    if e == BB:
                        pe.wait_ge(s_kt, 4)
                    if e % BB == 0 and k >= 2:
                        pe.wait_ge(s_y, k - 1)
                    o0 = (e % BB) * 64
                    tj = e // RB_[0]
                    v0 = V0[tj] + 2 * (e - R0[tj])
                    for g in range(G):
                        for hf in range(2):
                            mm(p_or[k % 2][HD * g:HD * (g + 1), o0:o0 + 64], vs[:, v0 + hf, HD * g:HD * (g + 1)],
                               pts[:, e % 2, hf, g // 2, (g % 2) * 64:(g % 2) * 64 + 64], start=(hf == 0), stop=(hf == 1))
                    mm(p_or[k % 2][:, o0 + 256:o0 + 320], amat[:, e % 2, :], const("hsel"), start=True, stop=True).then_inc(s_po, 1)
                f = b - 4
                if f >= 0 and f % BB == BB - 1:
                    n = f // BB
                    pe.wait_ge(s_ot, n + 1)
                    if n == 0:
                        pe.wait_ge(s_wo, 16)
                    for h in range(HH):
                        last = mm(p_or[n % 2][:, 0:D], ot[:, h, n % 2].rearrange("p b t -> p (b t)"),
                                  wo_sb[:, h, :], start=(h == 0), stop=(h == HH - 1))
                    last.then_inc(s_py, 1)


def kernel(**inputs):
    import numpy as _np
    import concourse.bacc as _bacc
    from concourse import mybir as _mybir
    from ml_dtypes import bfloat16 as _bf16
    from concourse.bass_utils import run_bass_kernel_spmd as _run

    g = {k: _np.ascontiguousarray(v) for k, v in inputs.items()}
    wq = g["L1_cond_Wq"].reshape(G, HH, HD, D).transpose(1, 0, 2, 3).reshape(H * HD, D)
    wo = g["L1_cond_Wo"].reshape(D, G, HH, HD).transpose(2, 1, 3, 0).reshape(H * HD, D)
    w_all = _np.concatenate([wq, g["L1_cond_Wk"], g["L1_cond_Wv"]], 0).T
    kv, cond = g["itok_B_37_3939"], g["itok_B_1_198"]
    row_meta = _np.concatenate([_np.repeat(a.reshape(NT, BB), T, axis=1).T for a in (kv, cond)]
                               + [_np.tile(kv, KK)[:, None]], 1)
    arrays = {
        "x": g["x"],
        "row_meta": row_meta,
        "tables": _np.tile(g["itok_Bx257_0_4111"], (KK, 1)),
        "w0": g["L0_cond_weights"].reshape(200 * T, T),
        "w_all": w_all,
        "wo_t": wo,
        "scales": _np.tile(_np.concatenate([g["L1_cond_q_norm_scale"], g["L1_cond_k_norm_scale"]])[None], (P, 1)),
        "kb": g["L1_cond_k_blocks"],
        "vb": g["L1_cond_v_blocks"],
        "consts": constants(),
        "sel": selectors().astype(_bf16),
    }
    arrays = {"in_" + k: _np.ascontiguousarray(v) for k, v in arrays.items()}
    nc = _bacc.Bacc("TRN2", target_bir_lowering=False, num_devices=1)
    args = [nc.dram_tensor(k, a.shape, _mybir.dt.from_np(a.dtype), kind="ExternalInput").ap() for k, a in arrays.items()]
    args.append(nc.dram_tensor("out_0", (B, T, D), F32, kind="ExternalOutput").ap())
    args.append(nc.dram_tensor("new_tab", (NJ * BLOCK, ROWF), F32, kind="Internal").ap())
    args.append(nc.dram_tensor("v_tab", (B * SP_, GD), F32, kind="Internal").ap())
    build(nc, *args)
    r = _run(nc, [arrays], core_ids=[0])
    return r.results[0]["out_0"]
```

```python
from contextlib import ExitStack

import concourse.bass as bass
import numpy as np
from concourse import mybir

F32 = mybir.dt.float32
BF16 = mybir.dt.bfloat16
I32 = mybir.dt.int32
ALU = mybir.AluOpType
ACT = mybir.ActivationFunctionType
AX_X = mybir.AxisListType.X

P = 128
B, T, D = 32, 32, 256
H, G, HD = 8, 4, 32
HH = H // G
BLOCK, NBLK, NPOOL = 16, 257, 4112
WINDOW = 128
SCALE = float(D) ** -0.5
EPS, THETA = 1e-6, 10000.0
GD = G * HD
BB = P // T
NT = B // BB
NS = 11
SP_ = NS * BLOCK
HS = SP_ // 2
KK = P // B
WS = 3
NJ = B * WS
RB = 8
NRT = B // RB
R0 = [j * RB for j in range(NRT)]
NR = RB * NS
NP_ = NT // 2
V0 = [(j % 2) * 2 * RB for j in range(NRT)]
K0 = [(j % 2) * RB * SP_ for j in range(NRT)]
NW = (H + 2 * G) * HD
BIG = 1.0e6
NEG = -1.0e30
MAGIC = 12582912.0
C1 = 6.28125
C2 = float(np.float32(np.round((2 * np.pi - C1) * 2 ** 21) / 2 ** 21))
C3 = float(np.float32(2 * np.pi - C1 - C2))
PI_ = 3.1415925

CONST_COLS = [("slot_of", 4), ("tcol", 1), ("iota", NBLK), ("ident", P), ("ones", P), ("pick_w", NT * WS),
              ("pick_r", B * NS), ("row_of", P), ("later", P), ("order", P), ("off16", BLOCK), ("cell", WS * BLOCK),
              ("bd", BB), ("eye", T), ("jrow", SP_), ("invf", HD // 2), ("eps", 1)]
CONST_AT = {}
_at = 0
for _name, _n in CONST_COLS:
    CONST_AT[_name] = (_at, _n)
    _at += _n
NCONST = _at
NFIRST = CONST_AT["ident"][0]
NEARLY = CONST_AT["jrow"][0]
MERGE_V = {b + q: (j, q) for j, b in ((1, 3), (2, 7), (3, 14)) for q in range(4)}
MERGE_K = {b + q: (j, q) for j, b in ((1, 0), (2, 10), (3, 18)) for q in range(4)}
KEYS_AT = {b + 1: jq for b, jq in MERGE_K.items()}
PROJECT_AT = {**{BB * (n + 1) + 5: n for n in range(NT - 2)}, B + 2: NT - 2, B + 4: NT - 1}


def constants():
    p = np.arange(P)
    kk, b = p // B, p % B
    c = {}
    c["ident"] = np.eye(P)
    c["ones"] = np.ones((P, P))
    c["slot_of"] = np.stack([kk, KK + kk, 2 * KK + kk, kk], 1)
    c["iota"] = np.tile(np.arange(NBLK), (P, 1))
    pw = np.zeros((P, NT, WS))
    for n in range(NT):
        for v in range(WS):
            pw[:, n, v] = (b // BB == n) & (kk == v)
    c["pick_w"] = pw.reshape(P, -1)
    r = np.arange(B * NS)
    c["pick_r"] = (b[:, None] == r // NS) & (kk[:, None] == r % NS % KK)
    c["row_of"] = b[:, None] % BB == p[None, :] // T
    order = np.where(kk < WS, WS * b + kk + 1, 0)
    c["order"] = np.tile(order, (P, 1))
    c["later"] = (order[:, None] > order[None, :]) & (order[None, :] > 0)
    c["cell"] = np.tile(np.arange(WS * BLOCK), (P, 1))
    c["off16"] = np.tile(np.arange(BLOCK), (P, 1))
    c["tcol"] = (p % T)[:, None]
    c["eye"] = p[:, None] % T == np.arange(T)[None, :]
    c["jrow"] = np.arange(SP_)[None, :] - (p % T)[:, None] + 63.5
    c["bd"] = p[:, None] // T == np.arange(BB)[None, :]
    c["invf"] = np.tile(1.0 / THETA ** (np.arange(HD // 2) / (HD // 2)), (P, 1))
    c["eps"] = np.full((P, 1), EPS)
    return np.concatenate([np.asarray(c[n], np.float32) for n, _ in CONST_COLS], 1)


def selectors():
    k, m = np.arange(P), np.arange(P)
    s = [(k[:, None] // T == j) & (k[:, None] % T == m[None, :] % T) for j in range(BB)]
    return np.concatenate(s, 1).astype(np.float32)


def build(nc, x, row_meta, tables, w0, w_all, wo_t, scales, kb, vb, consts, sel, out, new_tab, v_tab):
    with ExitStack() as ctx:
        def sb(name, shape, dt=F32):
            return ctx.enter_context(nc.sbuf_tensor(name, shape, dt))

        def sem(name):
            return ctx.enter_context(nc.semaphore(name))

        cst = sb("cst", [P, NCONST])

        def const(name):
            a, n = CONST_AT[name]
            return cst[:, a:a + n]

        ident, ones = const("ident"), const("ones")

        rm_i = sb("rm_i", [P, 2 * NT + 1], I32)
        rm = sb("rm", [P, 2 * NT + 1])
        kv_w, cond_w, kv = rm[:, 0:NT], rm[:, NT:2 * NT], rm[:, 2 * NT:2 * NT + 1]
        tab_i = sb("tab_i", [P, NBLK], I32)
        tab = sb("tab", [P, NBLK])
        scratch = sb("scratch", [P, 3 * NT * WS * BLOCK + NRT * P])
        ix = sb("ix", [P, 16])
        base = sb("base", [P, 4])
        found = sb("found", [P, 4])
        mv_w = sb("mv_w", [P, NT, WS])
        fl = sb("fl", [P, 3 * NT + 2])
        mv_j = sb("mv_j", [P, P])
        mv_r = sb("mv_r", [P, B + 1, NS])
        blk_rf = sb("blk_rf", [NR, NRT])
        rows_j = sb("rows_j", [P, P])
        blk_ri = sb("blk_ri", [NR, NRT], I32)
        cond_i = sb("cond_i", [P, NT], I32)
        cnt_rf = sb("cnt_rf", [NR, NRT])
        new_ri = sb("new_ri", [NR, NRT], I32)
        match = sb("match", [P, B, NS])
        cover = sb("cover", [P, BLOCK])
        cov_a = sb("cov_a", [P, 2, BLOCK])
        over = sb("over", [P, P])
        dcol = sb("dcol", [P, 2])
        dcell = sb("dcell", [P, 2, BLOCK])
        here = scratch[:, 0:NT * WS * BLOCK].rearrange("p (n c) -> p n c", c=WS * BLOCK)
        dwork = scratch[:, NT * WS * BLOCK:2 * NT * WS * BLOCK]
        dpick = scratch[:, 2 * NT * WS * BLOCK:3 * NT * WS * BLOCK]
        rwork = scratch[:, 3 * NT * WS * BLOCK:3 * NT * WS * BLOCK + NRT * P].rearrange("p (j c) -> p j c", c=P)
        wq8 = sb("wq8", [P, 4, NT])
        dst_i = sb("dst_i", [P, NT], I32)
        mask_c = sb("mask_c", [P, NT])
        sq_m = sb("sq_m", [P, 2, SP_])
        mask = sb("mask", [P, NT, SP_], BF16)
        selb = sb("selb", [P, BB, P], BF16)

        ang = sb("ang", [P, NT, HD // 2])
        turn = sb("turn", [P, NT, HD // 2])
        sin_ = sb("sin_", [P, NT, HD // 2])
        cos_ = sb("cos_", [P, NT, HD // 2])
        scl = sb("scl", [P, 2, HD])
        ga = sb("ga", [P, 2, HD])
        gb = sb("gb", [P, 2, HD])
        t1 = sb("t1", [P, 2, NT, HD])
        t2 = sb("t2", [P, 2, NT, HD])

        xs = sb("xs", [P, NT, D])
        x1 = xs
        wg = sb("wg", [P, NT, T])
        wbd = sb("wbd", [P, NT, BB, T])
        rows_kt = sb("rows_kt", [P, NT * D + 2 * NT * GD])
        xt = rows_kt[:, 0:NT * D].rearrange("p (n h f) -> p n h f", n=NT, h=2)
        new = rows_kt[:, NT * D:].rearrange("p (n c f) -> p n c f", c=2, f=GD)
        kt = rows_kt[:, 0:2 * RB * SP_]
        w_sb = sb("w_sb", [P, 2, NW])
        wo_sb = sb("wo_sb", [P, HH, D])
        sq = sb("sq", [P, 2 * H * HD])
        ra = sb("ra", [P, 2 * H * HD])
        rb = sb("rb", [P, 2 * H * HD])
        ms = sb("ms", [P, 2 * H])
        rt = sb("rt", [P, 2 * H])
        rstd = sb("rstd", [P, 2 * H])
        rq = sb("rq", [P, 2, 2 * H * HD])
        qbd = sb("qbd", [P, B, 2, P])

        k_old = sb("k_old", [P, 2, G * BLOCK * HD])
        v_old = sb("v_old", [P, 2, G * BLOCK * HD])
        mrg = sb("mrg", [P, 2, BLOCK, 2, GD])
        vs = sb("vs", [HS, 2 * 2 * RB, GD])

        keep = sb("keep", [NR, NRT, BLOCK], I32)

        pr = scratch[:, 0:3 * 2 * SP_].rearrange("p (c a s) -> p c a s", c=3, a=2)
        pts = sb("pts", [HS, 2, 2, 2, P])
        warm = sb("warm", [P, 1])
        nmx = sb("nmx", [P, 3, 2])
        sums = sb("sums", [P, 3, 2])
        rin = sb("rin", [P, 3, 2])
        ot = sb("ot", [P, HH, 2, BB, T])
        yo = sb("yo", [P, 2, D])

        psum = ctx.enter_context(nc.psum_tensor("psum", [P, 8, 512], F32))
        bank = [psum[:, i, :] for i in range(8)]
        p_ix = bank[1]
        p_rr = bank[7][:, 0:B * NS]
        p_xt, p_kv = [bank[2], bank[3]], [bank[4], bank[5]]
        p_q, p_qt, p_xr = [bank[2], bank[3]], [bank[6], bank[7]], bank[0]
        p_dw = bank[7][:, 0:NT * WS * BLOCK]
        p_s = [bank[b][:, 0:2 * SP_].rearrange("p (a s) -> p a s", a=2) for b in (2, 3)]
        p_pt, p_or = [bank[6], bank[7]], [bank[0], bank[1]]
        p_k = [bank[4], bank[5]]

        p_rj = p_ix[:, 0:P]
        p_br = p_ix[0:NR, 128:128 + NRT]
        p_cw = p_ix[:, 132:132 + BLOCK]
        p_ct = p_ix[:, 160:160 + NRT * BLOCK]

        s_rm = sem("s_rm"); s_tab = sem("s_tab"); s_c0 = sem("s_c0"); s_c1 = sem("s_c1"); s_c2 = sem("s_c2")
        s_x = sem("s_x"); s_w = sem("s_w"); s_wo = sem("s_wo"); s_scl = sem("s_scl"); s_sel = sem("s_sel")
        s_dve = sem("s_dve"); s_sh = sem("s_sh")
        s_ci = sem("s_ci")
        s_mvr = sem("s_mvr"); s_mvj = sem("s_mvj")
        s_br = sem("s_br"); s_ix = sem("s_ix"); s_rr = sem("s_rr")
        s_gi = sem("s_gi")
        s_nri = sem("s_nri"); s_mat = sem("s_mat"); s_cnt = sem("s_cnt")
        s_ovr = sem("s_ovr"); s_cw = sem("s_cw")
        s_dc = sem("s_dc"); s_dw = sem("s_dw"); s_dst = sem("s_dst")
        s_mc = sem("s_mc"); s_msq = sem("s_msq"); s_msk = sem("s_msk")
        s_ang = sem("s_ang"); s_trig = sem("s_trig")
        s_zero = sem("s_zero"); s_zr1 = sem("s_zr1"); s_init = sem("s_init")
        s_wg = [sem(f"s_wg{i}") for i in range(NT)]
        s_k = [sem(f"s_k{i}") for i in range(NRT)]
        s_v = [sem(f"s_v{i}") for i in range(NRT)]
        s_n = [sem(f"s_n{i}") for i in range(NRT)]
        s_sc = sem("s_sc")
        s_wbd = sem("s_wbd"); s_wbd2 = sem("s_wbd2"); s_we = sem("s_we")
        s_cos = sem("s_cos"); s_tq = sem("s_tq")
        s_pxt = sem("s_pxt"); s_xt = sem("s_xt"); s_pxr = sem("s_pxr"); s_x1 = sem("s_x1")
        s_pkv = sem("s_pkv"); s_vc = sem("s_vc"); s_ksum = sem("s_ksum"); s_kread = sem("s_kread")
        s_krt = sem("s_krt"); s_new = sem("s_new")
        s_pq = sem("s_pq"); s_qsq = sem("s_qsq"); s_qsum = sem("s_qsum"); s_qrt = sem("s_qrt"); s_rot = sem("s_rot")
        s_qread = sem("s_qread")
        s_pqt = sem("s_pqt"); s_qz = sem("s_qz"); s_qbd = sem("s_qbd")
        s_mv_ = sem("s_mrg_v"); s_mk = sem("s_mrg_k"); s_vst = sem("s_vst")
        s_vs = [sem(f"s_vs{i}") for i in range(NRT)]
        s_pk = sem("s_pk"); s_kt = sem("s_kt")
        s_ps = sem("s_ps"); s_nmx = sem("s_nmx"); s_pr = sem("s_pr"); s_ppt = sem("s_ppt"); s_pts = sem("s_pts")
        s_pn = sem("s_pn"); s_po = sem("s_po"); s_ot = sem("s_ot"); s_py = sem("s_py")
        s_y = sem("s_y"); s_out = [sem("s_out0"), sem("s_out1")]

        block = ctx.enter_context(nc.Block())

        @block.sync
        def _(sp):
            sp.dma_start(rm_i[:], row_meta).then_inc(s_rm, 16)
            sp.dma_start(cst[:, 0:NFIRST], consts[:, 0:NFIRST]).then_inc(s_c0, 16)
            sp.dma_start(tab_i[:], tables).then_inc(s_tab, 16)
            sp.dma_start(cst[:, NFIRST:NEARLY], consts[:, NFIRST:NEARLY]).then_inc(s_c1, 16)
            sp.dma_start(xs[:], x.rearrange("(n b) t d -> (b t) n d", b=BB)).then_inc(s_x, 16)
            sp.dma_start(cst[:, NEARLY:], consts[:, NEARLY:]).then_inc(s_c2, 16)
            sp.dma_start(w_sb[:], w_all.rearrange("(h p) n -> p h n", p=P)).then_inc(s_w, 16)
            sp.dma_start(scl[:], scales.rearrange("p (a b) -> p a b", a=2)).then_inc(s_scl, 16)
            sp.dma_start(selb[:].rearrange("p a b -> p (a b)"), sel).then_inc(s_sel, 16)
            sp.dma_start(wo_sb[:], wo_t.rearrange("(h p) n -> p h n", p=P)).then_inc(s_wo, 16)
            sp.wait_ge(s_zero, 1)
            sp.wait_ge(s_wg[NT - 1], 16)
            sp.dma_start(new_tab.rearrange("(j o) f -> j (o f)", o=BLOCK), mrg[0:NJ, 0].rearrange("p o c f -> p (o c f)")).then_inc(s_init, 16)
            out_v = out.rearrange("(n b) t d -> n (b t) d", b=BB)

            def rows_out(n):
                sp.wait_ge(s_y, n + 1)
                sp.dma_start(out_v[n], yo[:, n % 2, :]).then_inc(s_out[n % 2], 16)

            for j in range(NRT):
                if j == NRT - 1:
                    rows_out(0)
                    rows_out(1)
                sp.wait_ge(s_mv_, 4 * (j + 1))
                sp.dma_start(v_tab[R0[j] * SP_:(R0[j] + RB) * SP_, :].rearrange("(r o) f -> r o f", o=BLOCK),
                             mrg[0:NR, j % 2, :, 1, :]).then_inc(s_vst, 16)
                sp.wait_ge(s_vst, 16 * (j + 1))
                if j >= 2:
                    sp.wait_ge(s_po, R0[j - 1])
                sp.dma_start(vs[:, V0[j]:V0[j] + 2 * RB, :],
                             v_tab[R0[j] * SP_:(R0[j] + RB) * SP_, :].rearrange("(r p) f -> p r f", p=HS)
                             ).then_inc(s_vs[j], 16)
            for n in range(2, NT):
                rows_out(n)
            for i in range(2):
                sp.wait_ge(s_out[i], 16 * (NT // 2))

        @block.gpsimd
        def _(pool):
            nc.gpsimd.memset(mrg[:, 0], 0.0).then_inc(s_zero, 1)
            pool.wait_ge(s_ci, 1)
            for n in range(NT):
                pool.indirect_dma_start(wg[:, n, :], None, w0, bass.IndirectOffsetOnAxis(ap=cond_i[:, n:n + 1], axis=0),
                                        bounds_check=200 * T - 1, oob_is_err=False).then_inc(s_wg[n], 16)

            def gather_old(dst, src, j, s):
                pool.indirect_dma_start(dst[0:NR, j % 2, :], None, src.rearrange("n g o d -> n (g o d)"),
                                        bass.IndirectOffsetOnAxis(ap=blk_ri[0:NR, j:j + 1], axis=0),
                                        bounds_check=NPOOL - 1, oob_is_err=False).then_inc(s, 16)

            pool.wait_ge(s_gi, 1)
            for j in range(2):
                gather_old(v_old, vb, j, s_v[j])
                gather_old(k_old, kb, j, s_k[j])

            def window(n):
                pool.wait_ge(s_msq, n + 1)
                nc.gpsimd.tensor_scalar(mask[:, n, :], sq_m[:, n % 2, :], 64.0 * 64.0, NEG, ALU.is_gt, ALU.mult
                                        ).then_inc(s_msk, 1)

            pool.wait_ge(s_c2, 16)
            for n in range(NT // 2, NT):
                pool.wait_ge(s_wg[n], 16)
            nc.gpsimd.tensor_tensor(wg[:, NT // 2:, :], wg[:, NT // 2:, :],
                                    const("eye").unsqueeze(1).broadcast_to([P, NT // 2, T]), ALU.add).then_inc(s_we, 1)
            pool.wait_ge(s_we, 1)
            for n in range(NT // 2, NT):
                nc.gpsimd.tensor_tensor(wbd[:, n], wg[:, n, :].unsqueeze(1).broadcast_to([P, BB, T]),
                                        const("bd").unsqueeze(2).broadcast_to([P, BB, T]), ALU.mult).then_inc(s_wbd2, 1)
            for n in range(4):
                window(n)
            pool.wait_ge(s_cos, 1)
            for tt, gg, tr in ((t1, ga, cos_), (t2, gb, sin_)):
                nc.gpsimd.tensor_tensor(tt[:, 0].rearrange("p n (h i) -> p n h i", h=2),
                                        gg[:, 0].rearrange("p (h i) -> p h i", h=2).unsqueeze(1).broadcast_to([P, NT, 2, 16]),
                                        tr[:].unsqueeze(2).broadcast_to([P, NT, 2, 16]), ALU.mult).then_inc(s_tq, 1)

            def gather_new(j):
                pool.indirect_dma_start(mrg[0:NR, j % 2].rearrange("p o c f -> p (o c f)"), None,
                                        new_tab.rearrange("(j o) f -> j (o f)", o=BLOCK),
                                        bass.IndirectOffsetOnAxis(ap=new_ri[0:NR, j:j + 1], axis=0),
                                        bounds_check=NJ - 1, oob_is_err=False).then_inc(s_n[j], 16)

            pool.wait_ge(s_dst, 1)
            pool.wait_ge(s_init, 16)
            for n in range(NT):
                if n % 2 == 0:
                    pool.wait_ge(s_vc, n // 2 + 1)
                    pool.wait_ge(s_new, n // 2 + 1)
                pool.indirect_dma_start(new_tab, bass.IndirectOffsetOnAxis(ap=dst_i[:, n:n + 1], axis=0),
                                        new[:, n].rearrange("p c f -> p (c f)"), None,
                                        bounds_check=NJ * BLOCK - 1, oob_is_err=False).then_inc(s_sc, 16)
            pool.wait_ge(s_nri, 1)
            pool.wait_ge(s_sc, 16 * NT)
            gather_new(0)
            pool.wait_ge(s_zr1, 1)
            gather_new(1)

            def next_tile(j):
                pool.wait_ge(s_mk, 4 * (j - 1))
                gather_old(k_old, kb, j, s_k[j])
                pool.wait_ge(s_mv_, 4 * (j - 1))
                gather_old(v_old, vb, j, s_v[j])
                pool.wait_ge(s_vst, 16 * (j - 1))
                pool.wait_ge(s_pk, 4 * (j - 1))
                gather_new(j)

            next_tile(2)
            for n in range(4, NT):
                window(n)
            next_tile(3)

        @block.vector
        def _(dve):
            steps = [0]
            V = nc.vector

            def link(ins):
                steps[0] += 1
                ins.then_inc(s_dve, 1)
                dve.wait_ge(s_dve, steps[0])

            V.memset(mv_r[:, B, :], 0.0)
            dve.wait_ge(s_rm, 16)
            link(V.tensor_copy(rm[:], rm_i[:]))
            dve.wait_ge(s_c0, 16)
            V.tensor_scalar(wq8[:, 1, :], kv_w, const("tcol"), None, ALU.add)
            link(V.tensor_scalar(wq8[:, 0, :], cond_w, float(T), const("tcol"), ALU.mult, ALU.add))
            V.tensor_copy(cond_i[:], wq8[:, 0, :]).then_inc(s_ci, 1)
            V.tensor_scalar(fl[:, 0:NT], kv_w, 1.0 / BLOCK, -(WINDOW - 1) / BLOCK - 15 / 32, ALU.mult, ALU.add)
            V.tensor_scalar(fl[:, NT:2 * NT], kv_w, 1.0 / BLOCK, -15 / 32, ALU.mult, ALU.add)
            V.tensor_scalar(fl[:, 2 * NT:3 * NT], wq8[:, 1, :], 1.0 / BLOCK, -15 / 32, ALU.mult, ALU.add)
            V.tensor_scalar(fl[:, 3 * NT:3 * NT + 1], kv, 1.0 / BLOCK, -(WINDOW - 1) / BLOCK - 15 / 32, ALU.mult, ALU.add)
            link(V.tensor_scalar(fl[:, 3 * NT + 1:], kv, 1.0 / BLOCK, -15 / 32, ALU.mult, ALU.add))
            link(V.tensor_scalar(fl[:], fl[:], MAGIC, None, ALU.add))
            link(V.tensor_scalar(fl[:], fl[:], MAGIC, None, ALU.subtract))
            V.tensor_scalar(fl[:, 0:NT], fl[:, 0:NT], 0.0, None, ALU.max)
            link(V.tensor_scalar(fl[:, 3 * NT:3 * NT + 1], fl[:, 3 * NT:3 * NT + 1], 0.0, None, ALU.max))
            V.tensor_scalar(base[:, 0:3], const("slot_of")[:, 0:3], fl[:, 3 * NT:3 * NT + 1], None, ALU.add)
            V.tensor_scalar(base[:, 3:4], const("slot_of")[:, 3:4], fl[:, 3 * NT + 1:], None, ALU.add)
            dve.wait_ge(s_tab, 16)
            link(V.tensor_copy(tab[:], tab_i[:]))
            for i in range(4):
                last = V.scalar_tensor_tensor(out=scratch[:, i * NBLK:(i + 1) * NBLK], in0=const("iota"),
                                              scalar=base[:, i:i + 1], in1=tab[:],
                                              op0=ALU.is_equal, op1=ALU.mult, accum_out=found[:, i:i + 1])
            link(last)
            dve.wait_ge(s_c1, 16)
            pick_r = const("pick_r").rearrange("p (b s) -> p b s", s=NS)
            V.tensor_tensor(mv_r[:, 0:B, 0:2 * KK].rearrange("p b (i k) -> p b i k", k=KK),
                            pick_r[:, :, 0:2 * KK].rearrange("p b (i k) -> p b i k", k=KK),
                            found[:, 0:2].unsqueeze(1).unsqueeze(3).broadcast_to([P, B, 2, KK]), ALU.mult)
            V.tensor_tensor(mv_r[:, 0:B, 2 * KK:NS], pick_r[:, :, 2 * KK:NS],
                            found[:, 2:3].unsqueeze(2).broadcast_to([P, B, NS - 2 * KK]), ALU.mult).then_inc(s_mvr, 1)
            V.tensor_scalar(mv_j[:], ident, found[:, 3:4], None, ALU.mult).then_inc(s_mvj, 1)
            dve.wait_ge(s_br, 1)
            V.tensor_copy(blk_rf[:], p_br)
            V.tensor_copy(blk_ri[:], p_br).then_inc(s_gi, 1)
            dve.wait_ge(s_c2, 16)
            link(V.tensor_tensor(ang[:], wq8[:, 1, :].unsqueeze(2).broadcast_to([P, NT, HD // 2]),
                                 const("invf").unsqueeze(1).broadcast_to([P, NT, HD // 2]), ALU.mult))
            link(V.tensor_scalar(turn[:], ang[:], 1.0 / (2 * np.pi), MAGIC, ALU.mult, ALU.add))
            link(V.tensor_scalar(turn[:], turn[:], MAGIC, None, ALU.subtract))
            for c in (C1, C2, C3):
                link(V.scalar_tensor_tensor(out=ang[:], in0=turn[:], scalar=-c, in1=ang[:], op0=ALU.mult, op1=ALU.add))
            V.tensor_scalar(ang[:], ang[:], PI_, -PI_, ALU.min, ALU.max).then_inc(s_ang, 1)
            V.scalar_tensor_tensor(out=mask_c[:], in0=fl[:, 0:NT], scalar=float(BLOCK), in1=kv_w,
                                   op0=ALU.mult, op1=ALU.subtract).then_inc(s_mc, 1)
            dve.wait_ge(s_scl, 16)
            link(V.tensor_scalar(ga[:], scl[:], 1.0, None, ALU.add))
            link(V.tensor_scalar(ga[:, 0, :], ga[:, 0, :], SCALE, None, ALU.mult))
            V.tensor_copy(gb[:, :, 16:32], ga[:, :, 0:16])
            link(V.tensor_scalar(gb[:, :, 0:16], ga[:, :, 16:32], -1.0, None, ALU.mult))

            link(V.scalar_tensor_tensor(out=ix[:, 2:3], in0=base[:, 3:4], scalar=-float(BLOCK), in1=kv,
                                        op0=ALU.mult, op1=ALU.add))
            V.tensor_scalar(cov_a[:, 0, :], const("off16"), ix[:, 2:3], None, ALU.subtract)
            link(V.tensor_scalar(cov_a[:, 1, :], const("off16"), ix[:, 2:3], None, ALU.subtract))
            link(V.tensor_scalar(cov_a[:, 0, :], cov_a[:, 0, :], 0.0, None, ALU.is_ge))
            link(V.tensor_scalar(cov_a[:, 1, :], cov_a[:, 1, :], float(T), None, ALU.is_lt))
            link(V.tensor_tensor(cover[:], cov_a[:, 0, :], cov_a[:, 1, :], ALU.mult))

            def tables_of_rotation():
                dve.wait_ge(s_trig, 1)
                V.tensor_scalar(cos_[:], cos_[:], -2.0, 1.0, ALU.mult, ALU.add).then_inc(s_cos, 1)
                dve.wait_ge(s_cos, 1)
                for tt, gg, tr in ((t1, ga, cos_), (t2, gb, sin_)):
                    last = V.tensor_tensor(tt[:, 1].rearrange("p n (h i) -> p n h i", h=2),
                                           gg[:, 1].rearrange("p (h i) -> p h i", h=2).unsqueeze(1).broadcast_to([P, NT, 2, 16]),
                                           tr[:].unsqueeze(2).broadcast_to([P, NT, 2, 16]), ALU.mult)
                link(last)

            def wbd_tile(n):
                if n % 2 == 0:
                    dve.wait_ge(s_wg[n], 16)
                    dve.wait_ge(s_wg[n + 1], 16)
                    link(V.tensor_tensor(wg[:, n:n + 2, :], wg[:, n:n + 2, :],
                                         const("eye").unsqueeze(1).broadcast_to([P, 2, T]), ALU.add))
                V.tensor_tensor(wbd[:, n], wg[:, n, :].unsqueeze(1).broadcast_to([P, BB, T]),
                                const("bd").unsqueeze(2).broadcast_to([P, BB, T]), ALU.mult).then_inc(s_wbd, 1)

            def rotate(px, a, n, heads, s_sum, count, s_read, s_root):
                f = 2 * heads * HD
                av = ra[:, 0:f].rearrange("p (k h d) -> p k h d", k=2, d=HD)
                bv = rb[:, 0:f].rearrange("p (k h d) -> p k h d", k=2, d=HD)
                V.tensor_reduce(ms[:, 0:2 * heads], sq[:, 0:f].rearrange("p (h d) -> p h d", d=HD), AX_X,
                                ALU.add).then_inc(s_sum, 1)
                V.tensor_tensor(av, px, t1[:, a, n:n + 2, :].unsqueeze(2).broadcast_to([P, 2, heads, HD]), ALU.mult)
                V.tensor_tensor(bv[:, :, :, 0:16], px[:, :, :, 16:32],
                                t2[:, a, n:n + 2, 0:16].unsqueeze(2).broadcast_to([P, 2, heads, 16]), ALU.mult)
                V.tensor_tensor(bv[:, :, :, 16:32], px[:, :, :, 0:16],
                                t2[:, a, n:n + 2, 16:32].unsqueeze(2).broadcast_to([P, 2, heads, 16]), ALU.mult).then_inc(s_read, 1)
                dve.wait_ge(s_read, count)
                V.tensor_tensor(ra[:, 0:f], ra[:, 0:f], rb[:, 0:f], ALU.add)
                dve.wait_ge(s_root, count)
                link(V.reciprocal(rstd[:, 0:2 * heads], rt[:, 0:2 * heads]))
                return av, rstd[:, 0:2 * heads].rearrange("p (k h) -> p k h", k=2).unsqueeze(3).broadcast_to([P, 2, heads, HD])

            def keys_pair(i):
                if i >= 1:
                    dve.wait_ge(s_new, i)
                dve.wait_ge(s_vc, i + 1)
                av, rs = rotate(p_kv[i % 2][:].rearrange("p (k c h d) -> p k c h d", k=2, c=2, d=HD)[:, :, 0], 1, 2 * i, G,
                                s_ksum, i + 1, s_kread, s_krt)
                V.tensor_tensor(new[:, 2 * i:2 * i + 2, 0, :].rearrange("p k (h d) -> p k h d", d=HD), av, rs,
                                ALU.mult).then_inc(s_new, 1)

            def queries_pair(i):
                if i == 0:
                    dve.wait_ge(s_new, NP_)
                    dve.wait_ge(s_tq, 2)
                else:
                    dve.wait_ge(s_rot, i)
                dve.wait_ge(s_qsq, i + 1)
                if i >= 2:
                    dve.wait_ge(s_pqt, i - 1)
                av, rs = rotate(p_q[i % 2][:].rearrange("p (k h d) -> p k h d", k=2, d=HD), 0, 2 * i, H,
                                s_qsum, i + 1, s_qread, s_qrt)
                V.tensor_tensor(rq[:, i % 2, :].rearrange("p (k h d) -> p k h d", k=2, d=HD), av, rs, ALU.mult).then_inc(s_rot, 1)

            def over_index():
                dve.wait_ge(s_ix, 1)
                link(V.tensor_copy(rows_j[:], p_rj))
                V.scalar_tensor_tensor(out=over[:], in0=rows_j[:], scalar=found[:, 3:4], in1=const("later"),
                                       op0=ALU.is_equal, op1=ALU.mult).then_inc(s_ovr, 1)
                link(V.scalar_tensor_tensor(out=dwork[:, 0:P], in0=rows_j[:], scalar=found[:, 3:4], in1=const("order"),
                                            op0=ALU.is_equal, op1=ALU.mult))
                link(V.tensor_reduce(dcol[:, 0:1], dwork[:, 0:P], AX_X, ALU.max))
                link(V.tensor_scalar(dcol[:, 1:2], dcol[:, 0:1], float(BLOCK), -float(BLOCK), ALU.mult, ALU.add))
                link(V.tensor_scalar(dcell[:, 0, :], const("off16"), dcol[:, 1:2], None, ALU.add))
                link(V.scalar_tensor_tensor(out=wq8[:, 2, :], in0=fl[:, NT:2 * NT], scalar=-float(BLOCK), in1=wq8[:, 1, :],
                                            op0=ALU.mult, op1=ALU.add))
                V.tensor_tensor(here, const("cell").unsqueeze(1).broadcast_to([P, NT, WS * BLOCK]),
                                wq8[:, 2, :].unsqueeze(2).broadcast_to([P, NT, WS * BLOCK]), ALU.is_equal)
                dve.wait_ge(s_cw, 1)
                link(V.scalar_tensor_tensor(out=dcell[:, 1, :], in0=p_cw, scalar=BIG, in1=dcell[:, 0, :],
                                            op0=ALU.mult, op1=ALU.add))
                V.tensor_tensor(dwork.rearrange("p (v o) -> p v o", o=BLOCK),
                                const("pick_w").unsqueeze(2).broadcast_to([P, NT * WS, BLOCK]),
                                dcell[:, 1, :].unsqueeze(1).broadcast_to([P, NT * WS, BLOCK]), ALU.mult).then_inc(s_dc, 1)

            def rows_index():
                dve.wait_ge(s_dw, 1)
                link(V.tensor_tensor(dpick, here.rearrange("p n c -> p (n c)"), p_dw, ALU.mult))
                link(V.tensor_reduce(wq8[:, 3, :], dpick.rearrange("p (n c) -> p n c", c=WS * BLOCK), AX_X, ALU.add))
                V.tensor_copy(dst_i[:], wq8[:, 3, :]).then_inc(s_dst, 1)

            def match_index():
                dve.wait_ge(s_rr, 1)
                V.tensor_scalar(match[:], p_rr.rearrange("p (b s) -> p b s", s=NS), found[:, 3:4], None, ALU.is_equal
                                ).then_inc(s_mat, 1)

            def readers_index():
                link(V.tensor_tensor(rwork[0:NR], rows_j[0:NR].unsqueeze(1).broadcast_to([NR, NRT, P]),
                                     blk_rf[:].unsqueeze(2).broadcast_to([NR, NRT, P]), ALU.is_equal))
                link(V.tensor_tensor(rwork[0:NR], rwork[0:NR],
                                     const("order")[0:NR].unsqueeze(1).broadcast_to([NR, NRT, P]), ALU.mult))
                link(V.tensor_reduce(cnt_rf[:], rwork[0:NR], AX_X, ALU.max))
                link(V.tensor_scalar(blk_rf[:], cnt_rf[:], 0.0, BIG, ALU.is_equal, ALU.mult))
                link(V.scalar_tensor_tensor(out=blk_rf[:], in0=cnt_rf[:], scalar=-1.0, in1=blk_rf[:],
                                            op0=ALU.add, op1=ALU.add))
                V.tensor_copy(new_ri[:], blk_rf[:]).then_inc(s_nri, 1)

            def keep_masks():
                dve.wait_ge(s_cnt, 1)
                for j in range(NRT):
                    last = V.tensor_scalar(keep[0:NR, j, :], p_ct[0:NR, j * BLOCK:(j + 1) * BLOCK],
                                           0.0, None, ALU.is_equal)
                link(last)

            for n in range(4):
                wbd_tile(n)
            match_index()
            over_index()
            tables_of_rotation()
            rows_index()
            readers_index()
            for i in range(NP_):
                keys_pair(i)
            keep_masks()

            def merge(j, q, c, old, s_old, s_done):
                if q == 0:
                    dve.wait_ge(s_old, 16)
                    dve.wait_ge(s_n[j], 16)
                V.copy_predicated(mrg[0:NR, j % 2, 4 * q:4 * q + 4, c, :].rearrange("p o (g d) -> p o g d", d=HD),
                                  keep[0:NR, j, 4 * q:4 * q + 4].unsqueeze(2).unsqueeze(3).broadcast_to([NR, 4, G, HD]),
                                  old[0:NR, j % 2, :].rearrange("p (g o d) -> p o g d", g=G, d=HD)[:, 4 * q:4 * q + 4]
                                  ).then_inc(s_done, 1)

            def merge_values(j, q):
                merge(j, q, 1, v_old, s_v[j], s_mv_)

            def merge_keys(j, q):
                merge(j, q, 0, k_old, s_k[j], s_mk)

            def rows_out(n):
                dve.wait_ge(s_py, n + 1)
                if n >= 2:
                    dve.wait_ge(s_out[n % 2], 16 * (n // 2))
                V.tensor_tensor(yo[:, n % 2, :], p_or[n % 2][:, D:], x1[:, n, :], ALU.add).then_inc(s_y, 1)

            queries_pair(0)
            queries_pair(1)
            queries_pair(2)
            for q in range(4):
                merge_values(0, q)
            for q in range(4):
                merge_keys(0, q)
            queries_pair(3)
            for b in range(B + 5):
                if b < B:
                    dve.wait_ge(s_ps, b + 1)
                    if b >= 3:
                        dve.wait_ge(s_pr, 2 * (b - 2))
                    V.tensor_reduce(nmx[:, b % 3, :], p_s[b % 2], AX_X, ALU.max, negate=True).then_inc(s_nmx, 1)
                c = b - 1
                if 0 <= c < B:
                    dve.wait_ge(s_pr, 2 * c + 2)
                    link(V.reciprocal(rin[:, c % 3, :], sums[:, c % 3, :]))
                    for a in range(2):
                        V.tensor_scalar(pr[:, c % 3, a, :], pr[:, c % 3, a, :], rin[:, c % 3, a:a + 1], None, ALU.mult
                                        ).then_inc(s_pn, 1)
                if b in MERGE_K:
                    merge_keys(*MERGE_K[b])
                if b in MERGE_V:
                    merge_values(*MERGE_V[b])
                if b >= 2 * BB and b % BB == 2:
                    rows_out(b // BB - 2)
            rows_out(NT - 1)

        @block.scalar
        def _(act):
            A = nc.scalar

            A.memzero(qbd[:].rearrange("p b a f -> p (b a f)")).then_inc(s_qz, 1)
            act.wait_ge(s_ang, 1)
            A.activation(sin_[:], ang[:], ACT.Sin)
            A.activation(cos_[:], ang[:], ACT.Sin, scale=0.5).then_inc(s_sh, 1)
            act.wait_ge(s_sh, 1)
            A.activation(cos_[:], cos_[:], ACT.Square).then_inc(s_trig, 1)
            A.memzero(mrg[:, 1].rearrange("p o c f -> p (o c f)")).then_inc(s_zr1, 1)

            def window(n):
                if n == 0:
                    act.wait_ge(s_mc, 1)
                if n >= 2:
                    act.wait_ge(s_msk, n - 1)
                A.activation(sq_m[:, n % 2, :], const("jrow"), ACT.Square, bias=mask_c[:, n:n + 1]).then_inc(s_msq, 1)

            window(0)
            window(1)
            for i in range(NP_ + 1):
                if i < NP_:
                    act.wait_ge(s_pxt, i + 1)
                    A.activation(xt[:, 2 * i:2 * i + 2].rearrange("p k h f -> p (k h f)"), p_xt[i % 2][:], ACT.Copy).then_inc(s_xt, 1)
                    if i < 2:
                        window(2 + i)
                n = i - 1
                if 0 <= n:
                    act.wait_ge(s_pkv, n + 1)
                    if n >= 1:
                        act.wait_ge(s_ksum, n)
                    kv_ = p_kv[n % 2][:].rearrange("p (k c) -> p k c", k=2)
                    A.activation(sq[:, 0:2 * GD].rearrange("p (k c) -> p k c", k=2), kv_[:, :, 0:GD], ACT.Square)
                    A.activation(new[:, 2 * n:2 * n + 2, 1, :], kv_[:, :, GD:], ACT.Copy).then_inc(s_vc, 1)
                    act.wait_ge(s_ksum, n + 1)
                    if n >= 1:
                        act.wait_ge(s_new, n)
                    A.activation(rt[:, 0:2 * G], ms[:, 0:2 * G], ACT.Sqrt, scale=1.0 / HD, bias=const("eps")).then_inc(s_krt, 1)

            def queries_place(n):
                act.wait_ge(s_pqt, n + 1)
                if n == 0:
                    act.wait_ge(s_qz, 1)
                for g in range(G):
                    last = A.activation(
                        qbd[HD * g:HD * (g + 1), 2 * BB * n:2 * BB * (n + 1), g // 2, (g % 2) * 64:(g % 2) * 64 + 64
                            ].rearrange("p b (h t) -> p b h t", h=HH),
                        p_qt[n % 2][HD * g:HD * (g + 1), :].rearrange("p (h b t) -> p b h t", h=HH, b=2 * BB), ACT.Copy)
                last.then_inc(s_qbd, 1)

            def queries_square(i):
                act.wait_ge(s_pq, i + 1)
                if i >= 1:
                    act.wait_ge(s_qsum, i)
                A.activation(sq[:], p_q[i % 2][:], ACT.Square).then_inc(s_qsq, 1)

            def x1_by_rows(i):
                act.wait_ge(s_pxr, i + 1)
                A.activation(x1[:, 2 * i:2 * i + 2, :].rearrange("p k f -> p (k f)"), p_xr[:], ACT.Copy).then_inc(s_x1, 1)

            def queries_root(i):
                act.wait_ge(s_qsum, i + 1)
                if i == 0:
                    act.wait_ge(s_new, NP_)
                else:
                    act.wait_ge(s_rot, i)
                A.activation(rt[:, 0:2 * H], ms[:, 0:2 * H], ACT.Sqrt, scale=1.0 / HD, bias=const("eps")).then_inc(s_qrt, 1)

            for i in range(NP_ - 1):
                queries_square(i)
                x1_by_rows(i)
                queries_root(i)
                if i >= 1:
                    queries_place(i - 1)
            queries_square(NP_ - 1)
            x1_by_rows(NP_ - 1)
            queries_place(NP_ - 2)

            def keys(j, q):
                if j >= 2:
                    act.wait_ge(s_ps, R0[j - 1])
                act.wait_ge(s_pk, 4 * j + q + 1)
                A.activation(kt[:, K0[j]:K0[j] + RB * SP_].rearrange("p (r o) -> p r o", o=BLOCK)[:, :, 4 * q:4 * q + 4],
                             p_k[q % 2][:, 0:4 * NR].rearrange("p (o r) -> p r o", o=4), ACT.Copy).then_inc(s_kt, 1)

            for q in range(4):
                keys(0, q)
            queries_root(NP_ - 1)
            A.activation(warm[:], const("eps"), ACT.Exp)
            for b in range(B + 5):
                if b < B:
                    act.wait_ge(s_nmx, b + 1)
                    if b >= 3:
                        act.wait_ge(s_ppt, b - 2)
                    for a in range(2):
                        A.activation(pr[:, b % 3, a, :], p_s[b % 2][:, a], ACT.Exp,
                                     bias=nmx[:, b % 3, a:a + 1], accum_out=sums[:, b % 3, a:a + 1]).then_inc(s_pr, 1)
                c = b - 2
                if 0 <= c < B:
                    act.wait_ge(s_ppt, c + 1)
                    if c >= 2:
                        act.wait_ge(s_po, c - 1)
                    A.activation(pts[:, c % 2].rearrange("p a b f -> p (a b f)"), p_pt[c % 2][0:HS, :], ACT.Copy
                                 ).then_inc(s_pts, 1)
                if b in KEYS_AT:
                    keys(*KEYS_AT[b])
                k = (b - 3) // BB - 1
                if 0 <= k < NT and b % BB == 3:
                    act.wait_ge(s_po, BB * (k + 1))
                    if k >= 2:
                        act.wait_ge(s_py, k - 1)
                    A.activation(ot[:, :, k % 2].rearrange("p h b t -> p b h t"),
                                 p_or[k % 2][:, 0:D].rearrange("p (b h t) -> p b h t", b=BB, h=HH), ACT.Copy).then_inc(s_ot, 1)
                if b == 0:
                    queries_place(NP_ - 1)
                if 1 <= b <= 4:
                    window(3 + b)

        @block.tensor
        def _(pe):
            mm = pe.matmul
            pe.wait_ge(s_c1, 16)
            pe.wait_ge(s_mvr, 1)
            for j in range(NRT):
                last = mm(p_br[:, j:j + 1], mv_r[:, R0[j]:R0[j] + RB, :].rearrange("p b s -> p (b s)"), ones[:, 0:1],
                          start=True, stop=True)
            last.then_inc(s_br, 1)
            pe.wait_ge(s_mvj, 1)
            pe.wait_ge(s_gi, 1)
            mm(p_rj, ones, mv_j[:], start=True, stop=True).then_inc(s_ix, 1)
            mm(p_rr, ones, mv_r[:, 0:B, :].rearrange("p b s -> p (b s)"), start=True, stop=True).then_inc(s_rr, 1)

            def x1_pair(i):
                if i < NP_ // 2:
                    pe.wait_ge(s_wbd, 2 * i + 2)
                else:
                    pe.wait_ge(s_wbd2, 2 * i + 2 - NT // 2)
                if i >= 2:
                    pe.wait_ge(s_xt, i - 1)
                for n in (2 * i, 2 * i + 1):
                    for h in range(2):
                        o = p_xt[i % 2][:, (2 * (n % 2) + h) * P:(2 * (n % 2) + h + 1) * P]
                        last = mm(o, xs[:, n, h * P:(h + 1) * P], wbd[:, n].rearrange("p b t -> p (b t)"), start=True, stop=True)
                last.then_inc(s_pxt, 1)

            def project(o, n, c0, c1):
                for h in range(2):
                    last = mm(o, xt[:, n, h, :], w_sb[:, h, c0:c1], start=(h == 0), stop=(h == 1))
                return last

            def keys_values(i):
                pe.wait_ge(s_xt, i + 1)
                if i == 0:
                    pe.wait_ge(s_w, 16)
                if i >= 2:
                    pe.wait_ge(s_kread, i - 1)
                for k in range(2):
                    last = project(p_kv[i % 2][:, k * 2 * GD:(k + 1) * 2 * GD], 2 * i + k, H * HD, NW)
                last.then_inc(s_pkv, 1)

            def queries(i):
                if i == 0:
                    pe.wait_ge(s_xt, NP_)
                if i >= 2:
                    pe.wait_ge(s_qread, i - 1)
                for k in range(2):
                    last = project(p_q[i % 2][:, k * H * HD:(k + 1) * H * HD], 2 * i + k, 0, H * HD)
                last.then_inc(s_pq, 1)

            def x1_rows(i):
                if i >= 1:
                    pe.wait_ge(s_x1, i)
                for k in range(2):
                    for h in range(2):
                        last = pe.transpose(p_xr[:, (2 * k + h) * P:(2 * k + h + 1) * P], xt[:, 2 * i + k, h, :], ident)
                last.then_inc(s_pxr, 1)

            def queries_turn(i):
                pe.wait_ge(s_rot, i + 1)
                if i >= 2:
                    pe.wait_ge(s_qbd, i - 1)
                for k in range(2):
                    for h in range(HH):
                        last = pe.transpose(p_qt[i % 2][:, (2 * h + k) * P:(2 * h + k + 1) * P],
                                            rq[:, i % 2, (2 * k + h) * P:(2 * k + h + 1) * P], ident)
                last.then_inc(s_pqt, 1)

            pe.wait_ge(s_x, 16)
            x1_pair(0)
            pe.wait_ge(s_ovr, 1)
            mm(p_cw, over[:], cover[:], start=True, stop=True).then_inc(s_cw, 1)
            x1_pair(1)
            pe.wait_ge(s_mat, 1)
            pe.wait_ge(s_dc, 1)
            mm(p_dw, const("row_of"), dwork, start=True, stop=True).then_inc(s_dw, 1)
            keys_values(0)
            for j in range(NRT):
                last = mm(p_ct[0:NR, j * BLOCK:(j + 1) * BLOCK],
                          match[:, R0[j]:R0[j] + RB, :].rearrange("p b s -> p (b s)"), cover[:],
                          start=True, stop=True)
            last.then_inc(s_cnt, 1)
            x1_pair(2)
            keys_values(1)
            x1_pair(3)
            keys_values(2)
            keys_values(3)
            queries(0)
            x1_rows(0)
            queries(1)
            for i in range(NP_):
                if i + 2 < NP_:
                    queries(i + 2)
                if i + 1 < NP_:
                    queries_turn(i)
                    x1_rows(i + 1)

            def keys(j, q):
                pe.wait_ge(s_mk, 4 * j + q + 1)
                if 4 * j + q >= 2:
                    pe.wait_ge(s_kt, 4 * j + q - 1)
                for o in range(4):
                    last = pe.transpose(p_k[q % 2][:, o * NR:(o + 1) * NR],
                                        mrg[0:NR, j % 2, 4 * q + o, 0, :], ident[0:NR, 0:NR])
                last.then_inc(s_pk, 1)

            for q in range(4):
                keys(0, q)
            for b in range(B + 5):
                if b < B:
                    if b == 0:
                        pe.wait_ge(s_sel, 16)
                    if b % BB == 0:
                        pe.wait_ge(s_msk, b // BB + 1)
                    if b == 0:
                        pe.wait_ge(s_qbd, NP_ - 1)
                    if b in R0:
                        pe.wait_ge(s_kt, 4 * (R0.index(b) + 1))
                    if b >= 2:
                        pe.wait_ge(s_pr, 2 * (b - 1))
                    tj = b // RB
                    k0 = K0[tj] + (b - R0[tj]) * SP_
                    for a in range(2):
                        mm(p_s[b % 2][:, a], qbd[:, b, a, :], kt[:, k0:k0 + SP_], start=True, stop=False)
                        last = mm(p_s[b % 2][:, a], selb[:, b % BB, :], mask[:, b // BB, :], start=False, stop=True)
                    last.then_inc(s_ps, 1)
                if b == 0:
                    queries_turn(NP_ - 1)
                c = b - 2
                if 0 <= c < B:
                    pe.wait_ge(s_pn, 2 * c + 2)
                    if c == 1:
                        pe.wait_ge(s_qbd, NP_)
                    if c >= 2:
                        pe.wait_ge(s_pts, c - 1)
                    for hf in range(2):
                        for a in range(2):
                            k = 2 * hf + a
                            last = pe.transpose(p_pt[c % 2][0:HS, k * P:(k + 1) * P], pr[:, c % 3, a, hf * HS:(hf + 1) * HS], ident)
                    last.then_inc(s_ppt, 1)
                if b in KEYS_AT:
                    keys(*KEYS_AT[b])
                e = b - 3
                if 0 <= e < B:
                    pe.wait_ge(s_pts, e + 1)
                    if e in R0:
                        pe.wait_ge(s_vs[R0.index(e)], 16)
                    k = e // BB
                    if e % BB == 0 and k >= 2:
                        pe.wait_ge(s_y, k - 1)
                    o0 = (e % BB) * 64
                    tj = e // RB
                    v0 = V0[tj] + 2 * (e - R0[tj])
                    for g in range(G):
                        for hf in range(2):
                            last = mm(p_or[k % 2][HD * g:HD * (g + 1), o0:o0 + 64], vs[:, v0 + hf, HD * g:HD * (g + 1)],
                                      pts[:, e % 2, hf, g // 2, (g % 2) * 64:(g % 2) * 64 + 64], start=(hf == 0), stop=(hf == 1))
                    last.then_inc(s_po, 1)
                if b in PROJECT_AT:
                    n = PROJECT_AT[b]
                    pe.wait_ge(s_ot, n + 1)
                    if n == 0:
                        pe.wait_ge(s_wo, 16)
                    for h in range(HH):
                        last = mm(p_or[n % 2][:, D:], ot[:, h, n % 2].rearrange("p b t -> p (b t)"),
                                  wo_sb[:, h, :], start=(h == 0), stop=(h == HH - 1))
                    last.then_inc(s_py, 1)


def kernel(**inputs):
    import numpy as _np
    import concourse.bacc as _bacc
    from concourse import mybir as _mybir
    from ml_dtypes import bfloat16 as _bf16
    from concourse.bass_utils import run_bass_kernel_spmd as _run

    g = {k: _np.ascontiguousarray(v) for k, v in inputs.items()}
    wq = g["L1_cond_Wq"].reshape(G, HH, HD, D).transpose(1, 0, 2, 3).reshape(H * HD, D)
    wo = g["L1_cond_Wo"].reshape(D, G, HH, HD).transpose(2, 1, 3, 0).reshape(H * HD, D)
    w_all = _np.concatenate([wq, g["L1_cond_Wk"], g["L1_cond_Wv"]], 0).T
    kv, cond = g["itok_B_37_3939"], g["itok_B_1_198"]
    row_meta = _np.concatenate([_np.repeat(a.reshape(NT, BB), T, axis=1).T for a in (kv, cond)]
                               + [_np.tile(kv, KK)[:, None]], 1)
    arrays = {
        "x": g["x"],
        "row_meta": row_meta,
        "tables": _np.tile(g["itok_Bx257_0_4111"], (KK, 1)),
        "w0": g["L0_cond_weights"].reshape(200 * T, T),
        "w_all": w_all,
        "wo_t": wo,
        "scales": _np.tile(_np.concatenate([g["L1_cond_q_norm_scale"], g["L1_cond_k_norm_scale"]])[None], (P, 1)),
        "kb": g["L1_cond_k_blocks"],
        "vb": g["L1_cond_v_blocks"],
        "consts": constants(),
        "sel": selectors().astype(_bf16),
    }
    arrays = {"in_" + k: _np.ascontiguousarray(v) for k, v in arrays.items()}
    nc = _bacc.Bacc("TRN2", target_bir_lowering=False, num_devices=1)
    args = [nc.dram_tensor(k, a.shape, _mybir.dt.from_np(a.dtype), kind="ExternalInput").ap() for k, a in arrays.items()]
    args.append(nc.dram_tensor("out_0", (B, T, D), F32, kind="ExternalOutput").ap())
    args.append(nc.dram_tensor("new_tab", (NJ * BLOCK, 2 * GD), F32, kind="Internal").ap())
    args.append(nc.dram_tensor("v_tab", (B * SP_, GD), F32, kind="Internal").ap())
    build(nc, *args)
    r = _run(nc, [arrays], core_ids=[0])
    return r.results[0]["out_0"]
```
